# Optimizing a Trainium2 kernel written in Bass

```python
import numpy as np
import jax
import jax.numpy as jnp

def _softmax(x, axis=-1):
    return jax.nn.softmax(x, axis=axis)

def _gelu(x):
    return jax.nn.gelu(x, approximate=True)

def _silu(x):
    return jax.nn.silu(x)

def _sigmoid(x):
    return jax.nn.sigmoid(x)

def _layernorm(x, axis=-1, eps=1e-05):
    m = jnp.mean(x, axis=axis, keepdims=True)
    v = jnp.var(x, axis=axis, keepdims=True)
    return (x - m) / jnp.sqrt(v + eps)

def _scatter_add(tgt, idx, src, axis=0):
    return tgt.at[idx].add(src)

def _segment_sum(src, seg, n):
    return jax.ops.segment_sum(src, seg, n)
kernel_name = 'mk_decoder_postln_d2_seqx_r8_653d2b'

def setup_inputs(seed: int=0):
    np.random.seed(seed)
    _w = jnp.asarray

    def _rec_inputs():
        import jax
        import jax.numpy as jnp
        _rk = jax.random.key(seed)
        x = 0.5 + 0.2887 * jax.random.normal(jax.random.fold_in(_rk, 1), (4, 256, 256), jnp.float32)
        _lenS = 256 - jax.random.randint(jax.random.fold_in(_rk, 7), (4,), 0, max(1, 256 // 4) + 1, jnp.int32)
        _lenS2 = 256 - jax.random.randint(jax.random.fold_in(_rk, 8), (4,), 0, max(1, 256 // 4) + 1, jnp.int32)
        _ctx_512P = jax.random.normal(jax.random.fold_in(_rk, 11), (4, 16, 64), jnp.float32)
        _ctx_512c = jax.random.dirichlet(jax.random.fold_in(_rk, 511), 0.3 * jnp.ones((16,), jnp.float32), (4, 256))
        _ctx_512t = jnp.einsum('bsk,bkd->bsd', _ctx_512c, _ctx_512P)
        _ctx_512t = _ctx_512t * jax.lax.rsqrt(jnp.mean(jnp.square(_ctx_512t)) + 1e-12) * 0.953939
        ctx_512 = -0.000392918 + 0.999932 * (_ctx_512t + 0.3 * jax.random.normal(jax.random.fold_in(_rk, 611), (4, 256, 64), jnp.float32))
        return (x, ctx_512)
    x, ctx_512 = _rec_inputs()

    def _L0_attn_setup():
        import jax, jax.numpy as jnp
        import numpy as np
        HID = 256
        NH = 32
        QLR = 192
        KVLR = 64
        DR = 64
        DN = 128
        DV = 128
        DQK = DN + DR
        EPS = 1e-06
        ROPE_BASE = 10000.0

        def rms_norm(x, w):
            return x * jax.lax.rsqrt(jnp.mean(x * x, axis=-1, keepdims=True) + EPS) * w

        def apply_rope(x, pos):
            d = x.shape[-1]
            inv_freq = 1.0 / ROPE_BASE ** (jnp.arange(0, d, 2, dtype=jnp.float32) / d)
            freqs = pos[:, None].astype(jnp.float32) * inv_freq
            cos = jnp.cos(freqs)[None, :, None, :]
            sin = jnp.sin(freqs)[None, :, None, :]
            x1, x2 = (x[..., :d // 2], x[..., d // 2:])
            return jnp.concatenate([x1 * cos - x2 * sin, x1 * sin + x2 * cos], axis=-1)
        key = jax.random.key(seed)
        ks = jax.random.split(key, 8)
        s = 0.02
        return {'hidden_states': jax.random.normal(ks[0], (1, 256, HID), jnp.float32), 'q_a_w': jax.random.normal(ks[1], (HID, QLR), jnp.float32) * s, 'q_a_ln_w': jnp.ones((QLR,), jnp.float32), 'q_b_w': jax.random.normal(ks[2], (QLR, NH * DQK), jnp.float32) * s, 'kv_a_w': jax.random.normal(ks[3], (HID, KVLR + DR), jnp.float32) * s, 'kv_a_ln_w': jnp.ones((KVLR,), jnp.float32), 'kv_b_w': jax.random.normal(ks[4], (KVLR, NH * (DN + DV)), jnp.float32) * s, 'o_w': jax.random.normal(ks[5], (NH * DV, HID), jnp.float32) * s}
    _L0_attn_all = _L0_attn_setup()
    _L0_attn_in = {k: v for k, v in _L0_attn_all.items() if k in ('q_a_w', 'q_a_ln_w', 'q_b_w', 'kv_a_w', 'kv_a_ln_w', 'kv_b_w', 'o_w')}
    del _L0_attn_all

    def _L0_xattn_setup():
        import jax, jax.numpy as jnp
        import numpy as np
        B, N, D = (16, 256, 64)
        H = 4
        TOP_K_RATIO = 0.3
        key = jax.random.key(seed)
        k1, k2, k3, k4 = jax.random.split(key, 4)
        h = jax.random.normal(k1, (B, N, D), dtype=jnp.float32)
        adj_raw = jax.random.uniform(k2, (B, N, N), dtype=jnp.float32)
        lim = 1.0 / np.sqrt(D)
        Wq = jax.random.uniform(k3, (D, D), minval=-lim, maxval=lim, dtype=jnp.float32)
        Wk = jax.random.uniform(k4, (D, D), minval=-lim, maxval=lim, dtype=jnp.float32)
        gamma_raw = jnp.float32(-0.85)
        return {'h': h, 'adj_raw': adj_raw, 'Wq': Wq, 'Wk': Wk, 'gamma_raw': gamma_raw}
    _L0_xattn_all = _L0_xattn_setup()
    _L0_xattn_in = {k: v for k, v in _L0_xattn_all.items() if k in ('Wq', 'Wk', 'gamma_raw')}
    del _L0_xattn_all

    def _L0_ffn_setup():
        import jax, jax.numpy as jnp
        import numpy as np
        H = 256
        I = 256
        E_ROUTED = 7
        NS = 1
        TOPK = 2
        TEMP = 1.0

        def _moe_forward(x, Wr, br, gate_bias, Wup, bup, Wgate, bgate, Wdown, bdown, Wsu, bsu, Wsg, bsg, Wsd, bsd):
            B, S, _ = x.shape
            xt = x.reshape(-1, H)
            N = xt.shape[0]
            gate = (xt @ Wr + br) / TEMP
            bias_gate = gate + gate_bias
            _, ids = jax.lax.top_k(bias_gate, TOPK)
            sel_logits = jnp.take_along_axis(gate, ids, axis=-1)
            masked = jnp.full_like(gate, -jnp.inf)
            masked = masked.at[jnp.arange(N)[:, None], ids].set(sel_logits)
            probs = jax.nn.softmax(masked, axis=-1)
            u = jnp.einsum('nh,ehi->eni', xt, Wup) + bup[:, None, :]
            g = jax.nn.silu(jnp.einsum('eni,eij->enj', u, Wgate) + bgate[:, None, :]) * u
            eo = jnp.einsum('enj,ejh->enh', g, Wdown) + bdown[:, None, :]
            out = jnp.einsum('ne,enh->nh', probs, eo)
            su = (xt @ Wsu + bsu).reshape(N, NS, I)
            sg = jax.nn.silu(su @ Wsg + bsg) * su
            so = (sg @ Wsd + bsd).sum(axis=1)
            out = out + so
            return out.reshape(B, S, H)
        key = jax.random.key(seed)
        ks = jax.random.split(key, 20)
        s = lambda fan_in: 1.0 / np.sqrt(fan_in)
        inp = {'x': jax.random.normal(ks[0], (4, 128, H), dtype=jnp.float32), 'Wr': jax.random.normal(ks[1], (H, E_ROUTED), jnp.float32) * s(H), 'br': jax.random.normal(ks[2], (E_ROUTED,), jnp.float32) * s(H), 'gate_bias': jnp.zeros((E_ROUTED,), jnp.float32), 'Wup': jax.random.normal(ks[3], (E_ROUTED, H, I), jnp.float32) * s(H), 'bup': jax.random.normal(ks[4], (E_ROUTED, I), jnp.float32) * s(H), 'Wgate': jax.random.normal(ks[5], (E_ROUTED, I, I), jnp.float32) * s(I), 'bgate': jax.random.normal(ks[6], (E_ROUTED, I), jnp.float32) * s(I), 'Wdown': jax.random.normal(ks[7], (E_ROUTED, I, H), jnp.float32) * s(I), 'bdown': jax.random.normal(ks[8], (E_ROUTED, H), jnp.float32) * s(I), 'Wsu': jax.random.normal(ks[9], (H, NS * I), jnp.float32) * s(H), 'bsu': jax.random.normal(ks[10], (NS * I,), jnp.float32) * s(H), 'Wsg': jax.random.normal(ks[11], (I, I), jnp.float32) * s(I), 'bsg': jax.random.normal(ks[12], (I,), jnp.float32) * s(I), 'Wsd': jax.random.normal(ks[13], (I, H), jnp.float32) * s(I), 'bsd': jax.random.normal(ks[14], (H,), jnp.float32) * s(I)}
        return inp
    _L0_ffn_all = _L0_ffn_setup()
    _L0_ffn_in = {k: v for k, v in _L0_ffn_all.items() if k in ('Wr', 'br', 'gate_bias', 'Wup', 'bup', 'Wgate', 'bgate', 'Wdown', 'bdown', 'Wsu', 'bsu', 'Wsg', 'bsg', 'Wsd', 'bsd')}
    del _L0_ffn_all

    def _L1_attn_setup():
        import math
        import jax, jax.numpy as jnp
        import numpy as np
        B, S, D, H = (2, 256, 256, 16)
        HD = D // H
        ROPE_BASE = 10000.0

        def _rope_cos_sin(seqlen, dim):
            inv_freq = 1.0 / ROPE_BASE ** (jnp.arange(0, dim, 2, dtype=jnp.float32) / dim)
            t = jnp.arange(seqlen, dtype=jnp.float32)
            freqs = jnp.outer(t, inv_freq)
            return (jnp.cos(freqs), jnp.sin(freqs))
        key = jax.random.key(seed)
        k0, k1, k2 = jax.random.split(key, 3)
        return {'x': jax.random.normal(k0, (B, S, D), dtype=jnp.float32), 'Wqkv': jax.random.normal(k1, (D, 3 * D), dtype=jnp.float32) * 0.02, 'bqkv': jnp.zeros((3 * D,), dtype=jnp.float32), 'Wout': jax.random.normal(k2, (D, D), dtype=jnp.float32) * 0.02, 'bout': jnp.zeros((D,), dtype=jnp.float32)}
    _L1_attn_all = _L1_attn_setup()
    _L1_attn_in = {k: v for k, v in _L1_attn_all.items() if k in ('Wqkv', 'bqkv', 'Wout', 'bout')}
    del _L1_attn_all

    def _L1_xattn_setup():
        import jax, jax.numpy as jnp
        import numpy as np
        EPS = 1e-06
        IMAGE_DIMS = 256
        key = jax.random.key(seed)
        k1, k2, k3 = jax.random.split(key, 3)
        B, I, J, D = (16, 256, 256, 64)
        p = jax.random.normal(k1, (B, I, J), dtype=jnp.float32)
        k_v = jax.random.normal(k2, (B, J, D), dtype=jnp.float32)
        W_k = jax.random.normal(k3, (D, D), dtype=jnp.float32) * (1.0 / np.sqrt(D))
        b_k = jnp.zeros((D,), dtype=jnp.float32)
        ln_gamma = jnp.ones((J,), dtype=jnp.float32)
        ln_beta = jnp.zeros((J,), dtype=jnp.float32)
        return {'p': p, 'k_v': k_v, 'W_k': W_k, 'b_k': b_k, 'ln_gamma': ln_gamma, 'ln_beta': ln_beta}
    _L1_xattn_all = _L1_xattn_setup()
    _L1_xattn_in = {k: v for k, v in _L1_xattn_all.items() if k in ('W_k', 'b_k', 'ln_gamma', 'ln_beta')}
    del _L1_xattn_all

    def _L1_ffn_setup():
        import jax, jax.numpy as jnp
        import numpy as np
        DIM_IN = 256
        DIM_HIDDEN = 1024
        key = jax.random.key(seed)
        k_x, k_g, k_u, k_d = jax.random.split(key, 4)
        s_in = 1.0 / np.sqrt(DIM_IN)
        s_hid = 1.0 / np.sqrt(DIM_HIDDEN)
        x = jax.random.normal(k_x, (4, 256, DIM_IN), dtype=jnp.float32)
        w_gate = jax.random.uniform(k_g, (DIM_HIDDEN, DIM_IN), jnp.float32, -s_in, s_in)
        w_up = jax.random.uniform(k_u, (DIM_HIDDEN, DIM_IN), jnp.float32, -s_in, s_in)
        w_down = jax.random.uniform(k_d, (DIM_IN, DIM_HIDDEN), jnp.float32, -s_hid, s_hid)
        return {'x': x, 'w_gate': w_gate, 'w_up': w_up, 'w_down': w_down}
    _L1_ffn_all = _L1_ffn_setup()
    _L1_ffn_in = {k: v for k, v in _L1_ffn_all.items() if k in ('w_gate', 'w_up', 'w_down')}
    del _L1_ffn_all
    return {'x': x, 'ctx_512': ctx_512, 'L0_attn_q_a_w': _L0_attn_in['q_a_w'], 'L0_attn_q_a_ln_w': _L0_attn_in['q_a_ln_w'], 'L0_attn_q_b_w': _L0_attn_in['q_b_w'], 'L0_attn_kv_a_w': _L0_attn_in['kv_a_w'], 'L0_attn_kv_a_ln_w': _L0_attn_in['kv_a_ln_w'], 'L0_attn_kv_b_w': _L0_attn_in['kv_b_w'], 'L0_attn_o_w': _L0_attn_in['o_w'], 'L0_xattn_Wq': _L0_xattn_in['Wq'], 'L0_xattn_Wk': _L0_xattn_in['Wk'], 'L0_xattn_gamma_raw': _L0_xattn_in['gamma_raw'], 'L0_ffn_Wr': _L0_ffn_in['Wr'], 'L0_ffn_br': _L0_ffn_in['br'], 'L0_ffn_gate_bias': _L0_ffn_in['gate_bias'], 'L0_ffn_Wup': _L0_ffn_in['Wup'], 'L0_ffn_bup': _L0_ffn_in['bup'], 'L0_ffn_Wgate': _L0_ffn_in['Wgate'], 'L0_ffn_bgate': _L0_ffn_in['bgate'], 'L0_ffn_Wdown': _L0_ffn_in['Wdown'], 'L0_ffn_bdown': _L0_ffn_in['bdown'], 'L0_ffn_Wsu': _L0_ffn_in['Wsu'], 'L0_ffn_bsu': _L0_ffn_in['bsu'], 'L0_ffn_Wsg': _L0_ffn_in['Wsg'], 'L0_ffn_bsg': _L0_ffn_in['bsg'], 'L0_ffn_Wsd': _L0_ffn_in['Wsd'], 'L0_ffn_bsd': _L0_ffn_in['bsd'], 'L1_attn_Wqkv': _L1_attn_in['Wqkv'], 'L1_attn_bqkv': _L1_attn_in['bqkv'], 'L1_attn_Wout': _L1_attn_in['Wout'], 'L1_attn_bout': _L1_attn_in['bout'], 'L1_xattn_W_k': _L1_xattn_in['W_k'], 'L1_xattn_b_k': _L1_xattn_in['b_k'], 'L1_xattn_ln_gamma': _L1_xattn_in['ln_gamma'], 'L1_xattn_ln_beta': _L1_xattn_in['ln_beta'], 'L1_ffn_w_gate': _L1_ffn_in['w_gate'], 'L1_ffn_w_up': _L1_ffn_in['w_up'], 'L1_ffn_w_down': _L1_ffn_in['w_down']}

def reference(x, ctx_512, L0_attn_q_a_w, L0_attn_q_a_ln_w, L0_attn_q_b_w, L0_attn_kv_a_w, L0_attn_kv_a_ln_w, L0_attn_kv_b_w, L0_attn_o_w, L0_xattn_Wq, L0_xattn_Wk, L0_xattn_gamma_raw, L0_ffn_Wr, L0_ffn_br, L0_ffn_gate_bias, L0_ffn_Wup, L0_ffn_bup, L0_ffn_Wgate, L0_ffn_bgate, L0_ffn_Wdown, L0_ffn_bdown, L0_ffn_Wsu, L0_ffn_bsu, L0_ffn_Wsg, L0_ffn_bsg, L0_ffn_Wsd, L0_ffn_bsd, L1_attn_Wqkv, L1_attn_bqkv, L1_attn_Wout, L1_attn_bout, L1_xattn_W_k, L1_xattn_b_k, L1_xattn_ln_gamma, L1_xattn_ln_beta, L1_ffn_w_gate, L1_ffn_w_up, L1_ffn_w_down):
    import jax
    import jax.numpy as jnp

    def _L0_attn_ref(hidden_states, q_a_w, q_a_ln_w, q_b_w, kv_a_w, kv_a_ln_w, kv_b_w, o_w):
        import jax, jax.numpy as jnp
        import numpy as np
        HID = 256
        NH = 32
        QLR = 192
        KVLR = 64
        DR = 64
        DN = 128
        DV = 128
        DQK = DN + DR
        EPS = 1e-06
        ROPE_BASE = 10000.0

        def rms_norm(x, w):
            return x * jax.lax.rsqrt(jnp.mean(x * x, axis=-1, keepdims=True) + EPS) * w

        def apply_rope(x, pos):
            d = x.shape[-1]
            inv_freq = 1.0 / ROPE_BASE ** (jnp.arange(0, d, 2, dtype=jnp.float32) / d)
            freqs = pos[:, None].astype(jnp.float32) * inv_freq
            cos = jnp.cos(freqs)[None, :, None, :]
            sin = jnp.sin(freqs)[None, :, None, :]
            x1, x2 = (x[..., :d // 2], x[..., d // 2:])
            return jnp.concatenate([x1 * cos - x2 * sin, x1 * sin + x2 * cos], axis=-1)
        B, S, _ = hidden_states.shape
        q = rms_norm(hidden_states @ q_a_w, q_a_ln_w) @ q_b_w
        q = q.reshape(B, S, NH, DQK)
        q_pass, q_rot = (q[..., :DN], q[..., DN:])
        ckv = hidden_states @ kv_a_w
        c_kv, k_rot = (ckv[..., :KVLR], ckv[..., KVLR:])
        kv = rms_norm(c_kv, kv_a_ln_w) @ kv_b_w
        kv = kv.reshape(B, S, NH, DN + DV)
        k_pass, v = (kv[..., :DN], kv[..., DN:])
        pos = jnp.arange(S)
        q_rot = apply_rope(q_rot, pos)
        k_rot = apply_rope(k_rot[:, :, None, :], pos)[:, :, 0, :]
        scale = DQK ** (-0.5)
        scores = (jnp.einsum('bqhd,bkhd->bhqk', q_pass, k_pass) + jnp.einsum('bqhd,bkd->bhqk', q_rot, k_rot)) * scale
        causal = jnp.tril(jnp.ones((S, S), dtype=bool))
        scores = jnp.where(causal[None, None], scores, jnp.finfo(scores.dtype).min)
        p = jax.nn.softmax(scores, axis=-1)
        out = jnp.einsum('bhqk,bkhd->bqhd', p, v).reshape(B, S, NH * DV)
        return out @ o_w

    def _L0_xattn_ref(h, adj_raw, Wq, Wk, gamma_raw):
        import jax, jax.numpy as jnp
        import numpy as np
        B, N, D = (16, 256, 64)
        H = 4
        TOP_K_RATIO = 0.3
        b, n, dm = h.shape
        d = dm // H
        Q = (h @ Wq.T).reshape(b, n, H, d).transpose(0, 2, 1, 3)
        K = (h @ Wk.T).reshape(b, n, H, d).transpose(0, 2, 1, 3)
        sim = jnp.einsum('bhnd,bhmd->bnm', Q, K) / (jnp.sqrt(jnp.float32(d)) * H)
        k = max(1, int(n * TOP_K_RATIO))
        topk_vals = jax.lax.top_k(sim, k)[0]
        threshold = topk_vals[:, :, -1:]
        sparse_mask = (sim >= threshold).astype(sim.dtype)
        A_learned = jax.nn.sigmoid(sim) * sparse_mask
        A_learned = (A_learned + jnp.swapaxes(A_learned, -1, -2)) * 0.5
        gamma = jax.nn.sigmoid(gamma_raw)
        return (1.0 - gamma) * adj_raw + gamma * A_learned

    def _L0_ffn_ref(x, Wr, br, gate_bias, Wup, bup, Wgate, bgate, Wdown, bdown, Wsu, bsu, Wsg, bsg, Wsd, bsd):
        import jax, jax.numpy as jnp
        import numpy as np
        H = 256
        I = 256
        E_ROUTED = 7
        NS = 1
        TOPK = 2
        TEMP = 1.0

        def _moe_forward(x, Wr, br, gate_bias, Wup, bup, Wgate, bgate, Wdown, bdown, Wsu, bsu, Wsg, bsg, Wsd, bsd):
            B, S, _ = x.shape
            xt = x.reshape(-1, H)
            N = xt.shape[0]
            gate = (xt @ Wr + br) / TEMP
            bias_gate = gate + gate_bias
            _, ids = jax.lax.top_k(bias_gate, TOPK)
            sel_logits = jnp.take_along_axis(gate, ids, axis=-1)
            masked = jnp.full_like(gate, -jnp.inf)
            masked = masked.at[jnp.arange(N)[:, None], ids].set(sel_logits)
            probs = jax.nn.softmax(masked, axis=-1)
            u = jnp.einsum('nh,ehi->eni', xt, Wup) + bup[:, None, :]
            g = jax.nn.silu(jnp.einsum('eni,eij->enj', u, Wgate) + bgate[:, None, :]) * u
            eo = jnp.einsum('enj,ejh->enh', g, Wdown) + bdown[:, None, :]
            out = jnp.einsum('ne,enh->nh', probs, eo)
            su = (xt @ Wsu + bsu).reshape(N, NS, I)
            sg = jax.nn.silu(su @ Wsg + bsg) * su
            so = (sg @ Wsd + bsd).sum(axis=1)
            out = out + so
            return out.reshape(B, S, H)
        return _moe_forward(x, Wr, br, gate_bias, Wup, bup, Wgate, bgate, Wdown, bdown, Wsu, bsu, Wsg, bsg, Wsd, bsd)

    def _L1_attn_ref(x, Wqkv, bqkv, Wout, bout):
        import math
        import jax, jax.numpy as jnp
        import numpy as np
        B, S, D, H = (2, 256, 256, 16)
        HD = D // H
        ROPE_BASE = 10000.0

        def _rope_cos_sin(seqlen, dim):
            inv_freq = 1.0 / ROPE_BASE ** (jnp.arange(0, dim, 2, dtype=jnp.float32) / dim)
            t = jnp.arange(seqlen, dtype=jnp.float32)
            freqs = jnp.outer(t, inv_freq)
            return (jnp.cos(freqs), jnp.sin(freqs))
        b, s, d = x.shape
        hd = d // H
        qkv = (x @ Wqkv + bqkv).reshape(b, s, 3, H, hd)
        q, k, v = (qkv[:, :, 0], qkv[:, :, 1], qkv[:, :, 2])
        cos, sin = _rope_cos_sin(s, hd)
        c = cos[:, None, :]
        si = sin[:, None, :]

        def rot(t):
            t1, t2 = jnp.split(t.astype(jnp.float32), 2, axis=-1)
            return jnp.concatenate([t1 * c - t2 * si, t1 * si + t2 * c], axis=-1).astype(x.dtype)
        q = rot(q)
        k = rot(k)
        scale = 1.0 / math.sqrt(hd)
        scores = jnp.einsum('bthd,bshd->bhts', q, k * scale)
        causal_mask = jnp.triu(jnp.full((s, s), -10000.0, dtype=scores.dtype), 1)
        attn = jax.nn.softmax(scores + causal_mask, axis=-1)
        ctx = jnp.einsum('bhts,bshd->bthd', attn, v).reshape(b, s, d)
        return ctx @ Wout + bout

    def _L1_xattn_ref(p, k_v, W_k, b_k, ln_gamma, ln_beta):
        import jax, jax.numpy as jnp
        import numpy as np
        EPS = 1e-06
        IMAGE_DIMS = 256
        kv = k_v @ W_k.T + b_k
        out = jnp.einsum('bij,bjd->bid', p, kv)
        scale = IMAGE_DIMS ** (-0.5)
        sim = jnp.einsum('bid,bjd->bij', out, kv) * scale
        mu = jnp.mean(sim, axis=-1, keepdims=True)
        var = jnp.var(sim, axis=-1, keepdims=True)
        sim = (sim - mu) * jax.lax.rsqrt(var + EPS) * ln_gamma + ln_beta
        attn = jax.nn.softmax(sim, axis=-1)
        return attn

    def _L1_ffn_ref(x, w_gate, w_up, w_down):
        import jax, jax.numpy as jnp
        import numpy as np
        DIM_IN = 256
        DIM_HIDDEN = 1024
        gate = jnp.einsum('bsd,hd->bsh', x, w_gate)
        up = jnp.einsum('bsd,hd->bsh', x, w_up)
        gated = jax.nn.silu(gate) * up
        return jnp.einsum('bsh,dh->bsd', gated, w_down)
    x = _layernorm(x + _L0_attn_ref(x, L0_attn_q_a_w, L0_attn_q_a_ln_w, L0_attn_q_b_w, L0_attn_kv_a_w, L0_attn_kv_a_ln_w, L0_attn_kv_b_w, L0_attn_o_w), axis=-1)
    x = _layernorm(x + _L0_xattn_ref(ctx_512, x, L0_xattn_Wq, L0_xattn_Wk, L0_xattn_gamma_raw), axis=-1)
    x = _layernorm(x + _L0_ffn_ref(x, L0_ffn_Wr, L0_ffn_br, L0_ffn_gate_bias, L0_ffn_Wup, L0_ffn_bup, L0_ffn_Wgate, L0_ffn_bgate, L0_ffn_Wdown, L0_ffn_bdown, L0_ffn_Wsu, L0_ffn_bsu, L0_ffn_Wsg, L0_ffn_bsg, L0_ffn_Wsd, L0_ffn_bsd), axis=-1)
    x = _layernorm(x + _L1_attn_ref(x, L1_attn_Wqkv, L1_attn_bqkv, L1_attn_Wout, L1_attn_bout), axis=-1)
    x = _layernorm(x + _L1_xattn_ref(x, ctx_512, L1_xattn_W_k, L1_xattn_b_k, L1_xattn_ln_gamma, L1_xattn_ln_beta), axis=-1)
    x = _layernorm(x + _L1_ffn_ref(x, L1_ffn_w_gate, L1_ffn_w_up, L1_ffn_w_down), axis=-1)
    return x

_drawn_inputs = setup_inputs


def setup_inputs(seed=0):
    import zlib

    import numpy as np

    out = dict(_drawn_inputs(seed))
    spreads = {'L0_attn_q_a_ln_w': (1.0, 0.6),
     'L0_attn_kv_a_ln_w': (1.0, 0.2),
     'L0_ffn_gate_bias': (0.0, 0.1),
     'L1_attn_bqkv': (0.0, 0.1),
     'L1_attn_bout': (0.0, 0.1),
     'L1_xattn_b_k': (0.0, 0.8),
     'L1_xattn_ln_gamma': (1.0, 0.6),
     'L1_xattn_ln_beta': (0.0, 0.8)}
    factors = {'L0_attn_q_a_w': 4.504, 'L0_attn_q_b_w': 6.822, 'L1_xattn_W_k': 8.0}
    for name, (base, spread) in spreads.items():
        noise = np.random.default_rng([zlib.crc32(name.encode()), seed]).standard_normal(out[name].shape)
        drawn = base * np.exp(spread * noise) if base else spread * noise
        out[name] = jnp.asarray(drawn.astype(out[name].dtype))
    for name, factor in factors.items():
        out[name] = (out[name] * factor).astype(out[name].dtype)
    return out
```

```python
from contextlib import ExitStack

import numpy as np

import concourse.bass as bass
from concourse import mybir

F32 = mybir.dt.float32
F32R = mybir.dt.float32r
U32 = mybir.dt.uint32
I32 = mybir.dt.int32
ALU = mybir.AluOpType
ACT = mybir.ActivationFunctionType

P = 128
B, S, D = 4, 256, 256
T = B * S
NT = T // P
TB = S // P
DC = D // P
HALF = 512
NHALF = T // HALF
TH = HALF // P
CTX = 64

NH, QLR, KVLR, DR, DN, DV = 32, 192, 64, 64, 128, 128
KQ = QLR // 2
DQK = DN + DR
GH = 4
NG = NH // GH
NEG = -1.0e30

TOPK = int(S * 0.3)
E_ROUTED = 7
NE = E_ROUTED + 1

H1, HD1 = 16, 16
HS1 = 32
G1 = H1 // GH
HID = 1024
HT = HID // P
LN_EPS = 1e-5


class Queue:

    def __init__(self, sem):
        self.sem, self.count, self.todo, self.seen = sem, 0, [], {}

    def add(self, fn, *waits, signal=True):
        need = {}
        stack = list(waits)
        while stack:
            w = stack.pop()
            if w is None:
                continue
            if isinstance(w, list):
                stack.extend(w)
                continue
            sem, value = w
            if self.seen.get(id(sem), 0) < value:
                need[id(sem)] = (sem, max(value, need.get(id(sem), (sem, 0))[1]))
        for key, (sem, value) in need.items():
            self.seen[key] = value
        self.count += signal
        self.todo.append((list(need.values()), fn, signal))
        return (self.sem, self.count) if signal else None

    def play(self, eng):
        for waits, fn, signal in self.todo:
            for sem, value in waits:
                eng.wait_ge(sem, value)
            ins = fn(eng) if fn else None
            if signal:
                ins.then_inc(self.sem, 1)


class Slot:

    def __init__(self, t):
        self.t, self.free, self.taken = t, [], False

    def __setattr__(self, name, value):
        object.__setattr__(self, name, value)
        if name == "free":
            object.__setattr__(self, "taken", False)


class Ring:
    def __init__(self, slots):
        self.slots, self.at = slots, 0

    def next(self):
        s = self.slots[self.at % len(self.slots)]
        assert not s.taken, "its last user has not said when it is free"
        s.taken = True
        self.at += 1
        return s


class Pair:

    def __init__(self, hi, lo):
        self.hi, self.lo = hi, lo

    def __getitem__(self, key):
        return Pair(self.hi[key], self.lo[key])


def plain(ap):
    return ap.bitcast(F32)


def build(nc, a, out_dram):
    with ExitStack() as ctx:
        scope = [ctx]

        def sb(name, shape, dt=F32):
            return scope[0].enter_context(nc.sbuf_tensor(name, shape, dt))

        def stage_memory():
            scope[0] = ctx.enter_context(ExitStack())
            return scope[0]

        def sem(name):
            return ctx.enter_context(nc.semaphore(name))

        def ring(name, n, shape, dt=F32):
            return Ring([Slot(sb(f"{name}{i}", shape, dt)) for i in range(n)])

        def pair(name, shape):
            return Pair(sb(name + "_hi", shape, F32R), sb(name + "_lo", shape, F32R))

        def pair_ring(name, n, shape):
            return Ring([Slot(pair(f"{name}{i}", shape)) for i in range(n)])

        pe, act, dve, pool, sp = (Queue(sem(n)) for n in ("pe_done", "act_done", "dve_done", "pool_done", "sp_done"))
        banks = [Slot(ctx.enter_context(nc.psum_tensor(f"bank{i}", [P, 512], F32))) for i in range(8)]

        loads = [0]

        def load(pairs, *waits):
            done = sem(f"load{loads[0]}")
            loads[0] += 1
            for n, (dst, src) in enumerate(pairs):
                sp.add(lambda e, dst=dst, src=src: e.dma_start(dst, src).then_inc(done, 16),
                       *(waits if n == 0 else ()), signal=False)
            return (done, 16 * len(pairs))

        def mm(out, terms, *waits, start=True, stop=True, shared=False, signal=True):
            passes = []
            for lhsT, rhs in terms:
                if isinstance(lhsT, Pair):
                    passes += [(lhsT.hi, rhs.hi), (lhsT.hi, rhs.lo), (lhsT.lo, rhs.hi)]
                else:
                    passes.append((lhsT, rhs))
            for n, (lhsT, rhs) in enumerate(passes):
                first, last = n == 0, n == len(passes) - 1
                token = pe.add(
                    lambda e, lhsT=lhsT, rhs=rhs, s=start and first, z=stop and last: nc.tensor.matmul(
                        out, lhsT, rhs, start=s, stop=z, skip_group_check=shared),
                    *(waits if first else ()), signal=signal and last)
            return token

        def transpose(out, in_, *waits, signal=False):
            rows = in_.shape[0]
            return pe.add(lambda e: nc.tensor.transpose(out, in_, ident[0:rows, 0:rows]), *waits, signal=signal)

        def act_op(out, in_, func, *waits, **kw):
            return act.add(lambda e: e.activation(out, in_, func, **kw), *waits)

        def ts(q, out, in0, s1, s2, op0, op1, *waits):
            if op1 is None:
                return q.add(lambda e: e.tensor_scalar(out, in0, s1, None, op0), *waits)
            return q.add(lambda e: e.tensor_scalar(out, in0, s1, s2, op0, op1), *waits)

        def tt(q, out, in0, in1, op, *waits):
            return q.add(lambda e: e.tensor_tensor(out, in0, in1, op), *waits)

        def stt(q, out, in0, s, in1, op0, op1, *waits):
            return q.add(lambda e: e.scalar_tensor_tensor(out=out, in0=in0, scalar=s, in1=in1, op0=op0, op1=op1),
                         *waits)

        def split_psum(dst, src, *waits):
            hi = act_op(dst.hi, src, ACT.Copy, *waits)
            lo = tt(dve, dst.lo, src, plain(dst.hi), ALU.subtract, hi, *waits)
            return [hi, lo]

        def split_sbuf(dst, src, *waits):
            hi = act_op(dst.hi, src, ACT.Copy, *waits)
            lo = tt(pool, dst.lo, src, plain(dst.hi), ALU.subtract, hi, *waits)
            return [hi, lo]

        def last(q):
            return (q.sem, q.count)

        background, ready = [], {}

        def advance():
            if background:
                try:
                    next(background[0])
                except StopIteration:
                    background.pop(0)

        def need(key):
            while key not in ready:
                assert background, key
                advance()
            return ready[key]

        def pipeline(tasks, steps_of_background=1):
            running, wait = [], 0
            tasks = list(tasks)
            while tasks or running:
                while tasks and wait <= 0:
                    task, period = tasks.pop(0)
                    running.append(task)
                    wait = period
                    if period:
                        break
                wait -= 1
                for task in list(running):
                    try:
                        next(task)
                    except StopIteration:
                        running.remove(task)
                for _ in range(steps_of_background):
                    advance()

        ident = sb("identity", [P, P])
        iota = sb("iota", [P, NE])

        x = sb("x", [P, NT, D])
        y = sb("y", [P, NT, D])
        xT = sb("xT_plain", [P, DC, T])
        xT_pair = pair("xT", [P, DC, T])
        qaT = xT_pair[0:KQ, :, :]
        ctxT = sb("ctxT", [CTX, T])
        adjacency = sb("adjacency", [P, NT, D])
        kv_tok = sb("kv_tok", [P, NT, CTX])
        kvT = sb("kvT", [CTX, T])
        p_ring = ring("probs", 8, [P, 2 * S])
        pT_ring = ring("probsT", 6, [P, 2 * S])
        soft_ring = ring("soft", 12, [P, 3, 2])
        RAW, SPLIT = GH * (QLR + 2 * KVLR + D) + 2 * GH * DR, 3 * DC * D
        raw_ring = ring("w_raw", 2, [P, RAW])
        w_ring = pair_ring("w_split", 2, [P, SPLIT])
        gate_col = sb("gate_col", [P, 4])
        w_router = pair("w_router", [P, DC, NE])
        w_router_in = sb("w_router_in", [P, DC, NE])
        router_rows = sb("router_rows", [P, 2, NE])
        b_down = sb("b_down", [NE, D])
        b_up = sb("b_up", [P, NE, DC])
        b_gate = sb("b_gate", [P, NE, DC])
        router_ring = ring("router_buf", 2, [P, 4, TB, NE])
        rt_idx = ring("rt_idx", 2, [P, TB, NE], U32)
        rt_stat = ring("rt_stat", 2, [P, TB, NE])
        probs_e = sb("probs_e", [P, NT, NE])
        probs_eT_ring = ring("probs_eT", 2, [NE, S])
        stat_ring = ring("stat", 6, [P, 3, 2 * NT])
        bn_ring = ring("bn", 3, [P, NT, 8])

        proj = Ring(banks[0:2])
        score = Ring(banks[2:4])
        trans = Ring(banks[4:6])
        pv_bank, acc_bank = banks[6], banks[7]

        memory0 = stage_memory()
        mask0 = sb("mask0", [P, S])
        rope0 = sb("rope0", [P, TB, 2, DR])
        key_tok = sb("key_tok", [P, NT, KVLR + DR])
        keyT = sb("keyT", [P, T])
        qk_x = sb("qk_x", [CTX, 2, T])
        y_adj = sb("y_adj", [P, TB, S])
        sim_ring = ring("sim", 2, [P, 3, S])
        best_ring = ring("best", 2, [P, 8])
        w_qk_x = sb("w_qk_x", [CTX, 2, CTX])
        w_kv_x = sb("w_kv_x", [CTX, CTX])
        kv_bias_col = sb("kv_bias_col", [CTX, 1])
        kv_bias_row = sb("kv_bias_row", [P, CTX])
        memory_front = stage_memory()
        w_down0 = sb("w_down0", [P, DC, QLR + KVLR + DR])
        q_ln = sb("q_ln", [KQ, 2])
        kv_ln = sb("kv_ln", [P, KVLR])
        low = sb("low", [P, NT, QLR + KVLR + DR])
        sums = sb("sums", [P, 2, NT])
        square = sb("square", [P, 2, QLR])
        rope_tmp = sb("rope_tmp", [P, NT, 2, DR])

        l_xT = load([(xT[:, :, :], a["xT"].rearrange("(c p) t -> p c t", p=P))])
        l_low = load([(w_down0[:, :, 0:QLR], a["L0_attn_q_a_w"].rearrange("(c p) n -> p c n", p=P)),
                      (w_down0[:, :, QLR:], a["L0_attn_kv_a_w"].rearrange("(c p) n -> p c n", p=P))])
        raw0 = {}

        def raw_views(slot):
            t = slot.t
            cuts = np.cumsum([0, GH * QLR, GH * KVLR, 2 * GH * DR, GH * KVLR, GH * D])
            nope, k_lat, rot, v_lat, o = (slice(int(m), int(n)) for m, n in zip(cuts[:-1], cuts[1:]))
            return (t[:, nope].rearrange("p (h q) -> p h q", h=GH), t[:, k_lat].rearrange("p (h d) -> p h d", h=GH),
                    t[0:KQ, rot].rearrange("p (c h d) -> p c h d", c=2, h=GH),
                    t[:, v_lat].rearrange("p (h d) -> p h d", h=GH), t[:, o].rearrange("p (h n) -> p h n", h=GH))

        def load_group_weights(g):
            slot = raw_ring.next()
            nope, k_lat, rot, v_lat, o = raw_views(slot)
            h = slice(g * GH, (g + 1) * GH)
            w_q_in = load([(nope, a["w_nopeT"][:, h, :]), (k_lat, a["w_k_latT"][:, h, :])]
                          + [(rot[:, c, :, :], a["w_rot"][c * KQ:(c + 1) * KQ, h, :]) for c in range(2)], slot.free)
            w_v_in = load([(v_lat, a["w_v_latT"][:, h, :]), (o, a["w_o"][:, h, :])])
            raw0[g] = (slot, w_q_in, w_v_in)

        l_ident = load([(ident[:, :], a["identity"])])
        load_group_weights(0)
        l_const = load([(mask0[:, :], a["mask0"]),
                        (rope0[:, :, :, :], a["rope0"]), (q_ln[:, :], a["q_ln"]),
                        (kv_ln[:, :], a["L0_attn_kv_a_ln_w"].partition_broadcast(P))])
        l_x = load([(x[:, :, :], a["x"].rearrange("b (t p) d -> p (b t) d", p=P))])
        l_ctx = load([(ctxT[:, :], a["ctxT"])])
        l_x0 = load([(w_qk_x[:, 0, :], a["L0_xattn_WqT"]), (w_qk_x[:, 1, :], a["L0_xattn_WkT"]),
                     (gate_col[:, 0:1], a["gamma_raw"].partition_broadcast(P)),
                     (w_kv_x[:, :], a["L1_xattn_WkT"]), (kv_bias_col[:, :], a["L1_b_col"]),
                     (kv_bias_row[:, :], a["L1_xattn_b_k"].partition_broadcast(P))])
        load_group_weights(1)
        RSQRT_SEED, NEWTON_STEPS = float(0x5F3759DF), 3

        def rsqrt(v, n, eps, *waits):
            slot = stat_ring.next()
            ve, r, s = (slot.t[:, i, 0:n] for i in range(3))
            w_v = ts(dve, ve, v, eps, None, ALU.add, None, slot.free, *waits)
            w = ts(dve, r.bitcast(I32), ve.bitcast(I32), 1, None, ALU.logical_shift_right, None, w_v)
            w = ts(dve, r.bitcast(I32), r.bitcast(I32), -1.0, RSQRT_SEED, ALU.mult, ALU.add, w)
            for _ in range(NEWTON_STEPS):
                w = stt(dve, s, r, -0.5, r, ALU.mult, ALU.mult, w)
                w = tt(dve, s, s, ve, ALU.mult, w)
                w = stt(dve, r, s, 1.5, r, ALU.add, ALU.mult, w)
            return r, w, slot

        def layer_norm(src, dst, tiles, *waits, eps=LN_EPS):
            n = len(tiles)
            bn = bn_ring.next()
            w = bn.free
            for i, t in enumerate(tiles):
                w = [dve.add(lambda e, i=i, t=t: e.bn_stats(bn.t[:, i, 0:6], src(t)), w, *waits)]
            last_stats = w
            for i, t in enumerate(tiles):
                w = [dve.add(lambda e, i=i: e.bn_aggr(bn.t[:, i, 6:8], bn.t[:, i, 0:6]), last_stats)]
            r, w_r, slot = rsqrt(bn.t[:, 0:n, 7], n, eps, w)
            done = []
            for i, t in enumerate(tiles):
                done.append(ts(dve, dst(t), src(t), bn.t[:, i, 6:7], r[:, i:i + 1], ALU.subtract, ALU.mult,
                               w_r, *waits))
            slot.free = bn.free = done[-1:]
            return done

        def down_projections():
            w_copy = []
            for t in range(NT):
                bank = banks[t]
                w = mm(bank.t[:, 0:320], [(xT[:, c, t * P:(t + 1) * P], w_down0[:, c, :]) for c in range(DC)],
                       l_xT, l_low, bank.free)
                w_copy.append(act_op(low[:, t, :], bank.t[:, 0:320], ACT.Copy, w) if t % 2 == 0 else
                              dve.add(lambda e, t=t, bank=bank: e.tensor_copy(low[:, t, :], bank.t[:, 0:320]), w))
                bank.free = [w_copy[-1]]
            w_sq = None
            for t in range(NT):
                for i, (lo_, hi_) in enumerate(((0, QLR), (QLR, QLR + KVLR))):
                    part = low[:, t, lo_:hi_]
                    w_sq = dve.add(lambda e, part=part, i=i, t=t, n=hi_ - lo_: e.tensor_tensor_reduce(
                        out=square[:, i, 0:n], in0=part, in1=part, scale=1.0 / n, scalar=0.0,
                        op0=ALU.mult, op1=ALU.add, accum_out=sums[:, i, t:t + 1]), w_copy[t], w_sq)
            r, w_r, slot = rsqrt(sums[:, :, :].rearrange("p a t -> p (a t)"), 2 * NT, 1e-6, w_sq)
            w_qn, w_key = [], []
            tmp = rope_tmp
            for t in range(NT):
                w_qn.append(act_op(low[:, t, 0:QLR], low[:, t, 0:QLR], ACT.Copy, w_r, w_sq, w_copy[t],
                                   scale=r[:, t:t + 1]))
                w1 = stt(dve, key_tok[:, t, 0:KVLR], low[:, t, QLR:QLR + KVLR], r[:, NT + t:NT + t + 1],
                         kv_ln[:, :], ALU.mult, ALU.mult, w_r, l_const, w_copy[t])
                rot = low[:, t, QLR + KVLR:]
                pos = t % TB
                wa = tt(pool, tmp[:, t, 0, :], rot, rope0[:, pos, 0, :], ALU.mult, w_copy[t], l_const)
                hd = DR // 2
                tt(pool, tmp[:, t, 1, 0:hd], rot[:, hd:DR], rope0[:, pos, 1, 0:hd], ALU.mult)
                wb = tt(pool, tmp[:, t, 1, hd:DR], rot[:, 0:hd], rope0[:, pos, 1, hd:DR], ALU.mult)
                w2 = tt(pool, key_tok[:, t, KVLR:], tmp[:, t, 0, :], tmp[:, t, 1, :], ALU.add, wa, wb)
                w_key.append([w1, w2])
            slot.free = [w_qn[-1], w_key[-1][0]]
            w_qaT, w_keyT = [], []
            for h in range(NHALF):
                tiles = range(h * TH, (h + 1) * TH)
                for c in range(2):
                    bank = banks[2 * c + h]
                    for i, t in enumerate(tiles):
                        w = transpose(bank.t[0:KQ, i * P:(i + 1) * P], low[:, t, c * KQ:(c + 1) * KQ],
                                      w_qn[t], l_ident, bank.free, signal=True)
                    cols = slice(h * HALF, (h + 1) * HALF)
                    src = bank.t[0:KQ, :]
                    w_hi = act_op(qaT.hi[:, c, cols], src, ACT.Copy, w, l_const, scale=q_ln[:, c:c + 1])
                    w_lo = stt(dve, qaT.lo[:, c, cols], src, q_ln[:, c:c + 1], plain(qaT.hi[:, c, cols]),
                               ALU.mult, ALU.subtract, w_hi)
                    bank.free = [w_lo]
                    w_qaT += [w_hi, w_lo]
                bank = banks[4 + h]
                for i, t in enumerate(tiles):
                    w = transpose(bank.t[:, i * P:(i + 1) * P], key_tok[:, t, :], w_key[t], bank.free, signal=True)
                w_keyT.append(act_op(keyT[:, h * HALF:(h + 1) * HALF], bank.t[:, :], ACT.Copy, w))
                bank.free = [w_keyT[-1]]
            return w_qaT, w_keyT, [w for k in w_key for w in k]

        group_weights = {}

        def prepare_group_weights(g):
            slot, w_q_in, w_v_in = raw0[g]
            nope, k_lat, rot, v_lat, o = raw_views(slot)
            dst = w_ring.next()
            n_q = 2 * GH * P
            w_q = Pair(*(t[0:KQ, 0:n_q].rearrange("p (c h d) -> p c h d", c=2, h=GH) for t in (dst.t.hi, dst.t.lo)))
            w_out = Pair(*(t[:, n_q:].rearrange("p (j n) -> p j n", n=D) for t in (dst.t.hi, dst.t.lo)))
            w_rot = split_sbuf(w_q[:, :, :, KVLR:], rot, w_q_in, dst.free)
            bank = trans.next()
            out = bank.t[0:KQ, :].rearrange("p (c h d) -> p c h d", c=2, h=GH)
            for c in range(2):
                for i in range(GH):
                    w = mm(out[:, c, i, :], [(nope[:, i, c * KQ:(c + 1) * KQ], k_lat[:, i, :])], w_q_in, bank.free)
            w_abs = split_psum(w_q[:, :, :, 0:KVLR], out, w, dst.free)
            bank.free = w_abs[-1:]
            yield
            bank = trans.next()
            for i in range(GH):
                half = i % 2
                w = mm(bank.t[half * KVLR:(half + 1) * KVLR, (i // 2) * D:(i // 2 + 1) * D],
                       [(v_lat[:, i, :], o[:, i, :])], w_v_in, bank.free, shared=True)
            w_vo = split_psum(w_out[:, :, :], bank.t[:, :].rearrange("p (j n) -> p j n", n=D), w, dst.free)
            bank.free = w_vo[-1:]
            slot.free = [w] + w_rot
            group_weights[g] = (dst, w_q, w_out, w_rot + w_abs, w_vo)
            if g + 2 < NG:
                load_group_weights(g + 2)
            else:
                load_expert(g + 2 - NG)
                if g + 2 == NG:
                    background.append(load_experts_front())
            yield

        list(prepare_group_weights(0))
        w_qaT, w_keyT, w_key = down_projections()
        front_read = w_qaT + w_keyT + w_key
        memory_front.close()
        scope[0] = memory0
        q_tok_ring = ring("q_tok", 3, [P, GH, P])
        rope_ring = ring("rope_buf", 2, [P, 2, GH, DR])
        qT_ring = ring("qT", 3, [P, GH, S])
        ctx_pair_ring = pair_ring("ctx_pair", 2, [P, 2, S])
        for r in (q_tok_ring, rope_ring, qT_ring, ctx_pair_ring):
            for slot in r.slots:
                slot.free = list(front_read)
        SCALE0 = float(DQK) ** -0.5

        def exponentials(bank, w_scores, regions, scale):
            p, st = p_ring.next(), soft_ring.next()
            top, total = st.t[:, 0, :], st.t[:, 1, :]
            w_top, w_exp = [], []
            for i, (cols, mask) in enumerate(regions):
                w_top.append(dve.add(lambda e, i=i, cols=cols, mask=mask: e.tensor_tensor_reduce(
                    out=p.t[:, cols], in0=bank.t[:, cols], in1=mask, scale=-scale, scalar=3.0e38,
                    op0=ALU.add, op1=ALU.min, accum_out=top[:, i:i + 1]), w_scores, p.free, st.free))
            bank.free = w_top[-1:]
            for i, (cols, _) in enumerate(regions):
                w_exp.append(act_op(p.t[:, cols], p.t[:, cols], ACT.Exp, w_top[i], bias=top[:, i:i + 1], scale=-1.0,
                                    accum_out=total[:, i:i + 1]))
            return p, st, regions, w_exp

        def normalised(front):
            p, st, regions, w_exp = front
            inv = st.t[:, 2, :]
            w_inv = dve.add(lambda e: e.reciprocal(inv, st.t[:, 1, :]), w_exp)
            for i, (cols, _) in enumerate(regions):
                w = ts(pool, p.t[:, cols], p.t[:, cols], inv[:, i:i + 1], 1.0, ALU.mult, ALU.mult, w_inv)
            st.free = [w]
            return p, w

        y_token = {}

        def attention_group(b, g):
            tiles = [TB * b + i for i in range(TB)]
            w_slot, w_q, w_out, w_q_done, w_out_done = group_weights[g]
            qT = qT_ring.next()
            q_toks = []
            pbanks = [proj.next() for _ in tiles]
            for i, t in enumerate(tiles):
                bank = pbanks[i]
                w = w_proj = mm(bank.t[:, :],
                       [(qaT[:, c, t * P:(t + 1) * P], w_q[:, c, :, :]) for c in range(2)],
                       w_q_done, w_qaT, bank.free)
                q, rp = q_tok_ring.next(), rope_ring.next()
                view = bank.t[:, :].rearrange("p (h d) -> p h d", d=P)
                lat, rot = view[:, :, 0:KVLR], view[:, :, KVLR:]
                hd = DR // 2
                cos = rope0[:, i, 0, :].unsqueeze(1).to_broadcast([P, GH, DR])
                sin_lo = rope0[:, i, 1, 0:hd].unsqueeze(1).to_broadcast([P, GH, hd])
                sin_hi = rope0[:, i, 1, hd:DR].unsqueeze(1).to_broadcast([P, GH, hd])
                w1 = tt(dve, rp.t[:, 0, :, :], rot, cos, ALU.mult, w, rp.free)
                tt(dve, rp.t[:, 1, :, 0:hd], rot[:, :, hd:DR], sin_lo, ALU.mult)
                w2 = tt(dve, rp.t[:, 1, :, hd:DR], rot[:, :, 0:hd], sin_hi, ALU.mult)
                w_rot = tt(pool, q.t[:, :, KVLR:], rp.t[:, 0, :, :], rp.t[:, 1, :, :], ALU.add, w1, w2, q.free)
                rp.free = [w_rot]
                w_lat = act_op(q.t[:, :, 0:KVLR], lat, ACT.Copy, w, w2, q.free)
                bank.free = [w_lat]
                q_toks.append((q, w_lat, w_rot))
            if g == NG - 1:
                xT_free[b] = [w_proj]
            yield
            w_qT = []
            for i, (q, w_lat, w_rot) in enumerate(q_toks):
                bank = pbanks[i]
                for h in range(GH):
                    w = transpose(bank.t[:, h * P:(h + 1) * P], q.t[:, h, :], w_lat, w_rot, bank.free,
                                  signal=h == GH - 1)
                q.free = [w]
                w_qT.append(act_op(qT.t[:, :, i * P:(i + 1) * P], bank.t[:, :].rearrange("p (h s) -> p h s", s=P),
                                   ACT.Copy, w, qT.free))
                bank.free = [w_qT[-1]]
            yield
            fronts, probs = [], []
            keys = keyT[:, b * S:(b + 1) * S]
            for h in range(GH):
                bank = score.next()
                mm(bank.t[:, 0:S], [(qT.t[:, h, P:S], keys)], w_qT, w_keyT, bank.free, signal=False)
                w = mm(bank.t[:, S:S + P], [(qT.t[:, h, 0:P], keys[:, 0:P])])
                fronts.append(exponentials(bank, w, [(slice(0, S), mask0[:, :]), (slice(S, S + P), mask0[:, P:S])],
                                           SCALE0))
                if h == 1:
                    yield
            qT.free = [w]
            probs += [normalised(f) for f in fronts[:2]]
            yield
            probs += [normalised(f) for f in fronts[2:]]
            pTs = []
            for h, (p, w_p) in enumerate(probs):
                bank, pT = trans.next(), pT_ring.next()
                transpose(bank.t[:, 0:P], p.t[:, S:S + P], w_p, bank.free)
                transpose(bank.t[:, P:2 * P], p.t[:, 0:P])
                w = transpose(bank.t[:, 2 * P:3 * P], p.t[:, P:S], signal=True)
                p.free = [w]
                w = dve.add(lambda e, pT=pT, bank=bank: e.tensor_copy(pT.t[:, 0:3 * P], bank.t[:, 0:3 * P]),
                            w, pT.free)
                bank.free = [w]
                pTs.append((pT, w))
                if h == 1:
                    yield
            yield
            bank = pv_bank
            for h, (pT, w_pT) in enumerate(pTs):
                out = bank.t[(h % 2) * KVLR:(h % 2 + 1) * KVLR, (h // 2) * S:(h // 2 + 1) * S]
                mm(out, [(key_tok[:, tiles[0], 0:KVLR], pT.t[:, 0:S])], w_pT, w_key, bank.free,
                   stop=False, shared=True, signal=False)
                w = mm(out[:, P:S], [(key_tok[:, tiles[1], 0:KVLR], pT.t[:, S:S + P])], start=False, shared=True)
                pT.free = [w]
            ctxp = ctx_pair_ring.next()
            w_ctx = split_psum(Pair(ctxp.t.hi[:, :, :], ctxp.t.lo[:, :, :]),
                               bank.t[:, :].rearrange("p (a s) -> p a s", s=S), w, ctxp.free)
            bank.free = w_ctx[-1:]
            yield
            for i in range(TB):
                terms = [(ctxp.t[:, j, i * P:(i + 1) * P], w_out[:, j, :]) for j in range(2)]
                w = mm(acc_bank.t[:, i * D:(i + 1) * D], terms, w_ctx, w_out_done, acc_bank.free)
            ctxp.free = [w]
            if b == B - 1:
                w_slot.free = [w]
            rows = slice(TB * b, TB * b + TB)
            before = x if g == 0 else y
            y_token[b] = tt(dve, y[:, rows, :], acc_bank.t[:, :].rearrange("p (t d) -> p t d", d=D),
                            before[:, rows, :], ALU.add, w, l_x, y_token.get(b))
            acc_bank.free = [y_token[b]]
            if g == NG - 1:
                background.append(finish_attention0(b, y_token[b]))
            yield

        gate_tokens = []

        def learned_adjacency():
            w = act_op(gate_col[:, 1:2], gate_col[:, 0:1], ACT.Exp, l_x0, scale=-1.0)
            w = ts(dve, gate_col[:, 1:2], gate_col[:, 1:2], 1.0, None, ALU.add, None, w)
            w = dve.add(lambda e: e.reciprocal(gate_col[:, 1:2], gate_col[:, 1:2]), w)
            w1 = ts(dve, gate_col[:, 2:3], gate_col[:, 1:2], 0.5, None, ALU.mult, None, w)
            w2 = ts(dve, gate_col[:, 3:4], gate_col[:, 1:2], -1.0, 1.0, ALU.mult, ALU.add, w)
            gate_tokens.extend([w1, w2])
            w_qk = []
            for i in range(2):
                for h in range(NHALF):
                    bank = trans.next()
                    cols = slice(h * HALF, (h + 1) * HALF)
                    w = mm(bank.t[0:CTX, :], [(w_qk_x[:, i, :], ctxT[:, cols])], l_x0, l_ctx, bank.free)
                    w_qk.append(act_op(qk_x[:, i, cols], bank.t[0:CTX, :], ACT.Copy, w))
                    bank.free = w_qk[-1:]
                yield
            for b in range(B):
                w_adj, rows = [], []
                for i in range(TB):
                    t = TB * b + i
                    s, best, bank = sim_ring.next(), best_ring.next(), trans.next()
                    w = mm(bank.t[:, 0:S], [(qk_x[:, 0, t * P:(t + 1) * P], qk_x[:, 1, b * S:(b + 1) * S])],
                           w_qk, bank.free)
                    sim, work, sig = s.t[:, 0, :], s.t[:, 1, :], s.t[:, 2, :]
                    w_sim = act_op(sim, bank.t[:, 0:S], ACT.Copy, w, s.free)
                    bank.free = [w_sim]
                    w_sig = act_op(sig, sim, ACT.Exp, w_sim, s.free, scale=-1.0 / 16)
                    rows.append([s, best, sim, work, sig, w_sim, w_sig])
                yield
                for k in range((TOPK - 1) // 8 + 1):
                    for row in rows:
                        s, best, sim, work, _, w, _ = row
                        src = work if k else sim
                        row[5] = dve.add(lambda e, src=src, best=best: e.max(best.t[:, :], src), w, best.free, s.free)
                    if k < (TOPK - 1) // 8:
                        for row in rows:
                            s, best, sim, work, _, w, _ = row
                            src = work if k else sim
                            row[5] = dve.add(lambda e, src=src, work=work, best=best: e.match_replace(
                                out=work, in_to_replace=best.t[:, :], in_values=src, imm_value=-3.0e38), w)
                    yield
                for i, (s, best, sim, work, sig, w, w_sig) in enumerate(rows):
                    w_sig = ts(dve, sig, sig, 1.0, None, ALU.add, None, w_sig)
                    w_sig = dve.add(lambda e, sig=sig: e.reciprocal(sig, sig), w_sig)
                    at = (TOPK - 1) % 8
                    w = stt(dve, y_adj[:, i, :], sim, best.t[:, at:at + 1], sig, ALU.is_ge, ALU.mult,
                            w, w_sig, adj_free)
                    s.free = best.free = [w]
                    w_adj.append(w)
                yield
                bank = trans.next()
                for i in range(TB):
                    for j in range(TB):
                        w = transpose(bank.t[:, i * S + j * P:i * S + (j + 1) * P], y_adj[:, j, i * P:(i + 1) * P],
                                      w_adj, bank.free, signal=True)
                rows = slice(TB * b, TB * b + TB)
                w = tt(dve, adjacency[:, rows, :], bank.t[:, :].rearrange("p (t d) -> p t d", d=S), y_adj[:, :, :],
                       ALU.add, w)
                bank.free = [w]
                adj_free[:] = [w]
                ready["adjacency", b] = w
                yield
            ready["adjacency_done"] = True

        adj_free = []

        def context_keys():
            bank = trans.next()
            view = bank.t[:, :].rearrange("p (t d) -> p t d", d=CTX)
            for t in range(NT):
                w = mm(view[:, t, :], [(ctxT[:, t * P:(t + 1) * P], w_kv_x[:, :])], l_x0, l_ctx, bank.free,
                       signal=t == NT - 1)
            w1 = tt(dve, kv_tok[:, :, :], view, kv_bias_row[:, :].unsqueeze(1).to_broadcast([P, NT, CTX]), ALU.add, w)
            bank.free = [w1]
            tokens = [w1]
            yield
            for h in range(NHALF):
                bank = trans.next()
                cols = slice(h * HALF, (h + 1) * HALF)
                w = mm(bank.t[0:CTX, :], [(w_kv_x[:, :], ctxT[:, cols])], bank.free)
                tokens.append(act_op(kvT[:, cols], bank.t[0:CTX, :], ACT.Identity, w, bias=kv_bias_col[:, 0:1]))
                bank.free = tokens[-1:]
            ready["context_keys"] = tokens
            yield

        xT_free = [[] for _ in range(B)]

        def transpose_x(b, w_x, dst=None):
            bank = trans.next()
            for c in range(DC):
                for i in range(TB):
                    w = transpose(bank.t[:, c * S + i * P:c * S + (i + 1) * P],
                                  x[:, TB * b + i, c * P:(c + 1) * P], w_x, bank.free, signal=True)
            cols = slice(b * S, (b + 1) * S)
            view = bank.t[:, :].rearrange("p (c s) -> p c s", s=S)
            if dst is not None:
                tokens = [act_op(dst[:, :, cols], view, ACT.Copy, w, xT_free[b])]
            else:
                tokens = split_psum(Pair(xT_pair.hi[:, :, cols], xT_pair.lo[:, :, cols]), view, w, xT_free[b])
            bank.free = tokens[-1:]
            return tokens

        def x_tile(t):
            return x[:, t, :]

        def y_tile(t):
            return y[:, t, :]

        def finish_attention0(b, w_y):
            tiles = [TB * b + i for i in range(TB)]
            w_x = layer_norm(y_tile, x_tile, tiles, w_y)
            yield
            w_adj = need_inner(("adjacency", b))
            w_mix = []
            for t in tiles:
                w = stt(dve, y[:, t, :], x[:, t, :], gate_col[:, 3:4], x[:, t, :], ALU.mult, ALU.add,
                        w_x, gate_tokens)
                w_mix.append(stt(dve, y[:, t, :], adjacency[:, t, :], gate_col[:, 2:3], y[:, t, :],
                                 ALU.mult, ALU.add, w, w_adj))
            yield
            w_x = layer_norm(y_tile, x_tile, tiles, w_mix)
            yield
            ready["xT_experts", b] = transpose_x(b, w_x)
            ready["x_experts", b] = w_x
            yield
            yield from router(b)

        def need_inner(key):
            assert key in ready, key
            return ready[key]

        w_e_loaded, w_e_ready = {}, {}

        def expert_views(t, lead=3):
            return t[:, 0:3 * DC * D].rearrange("p (i c n) -> p i c n", i=3, c=DC)

        def load_expert(e):
            slot = raw_ring.next()
            view = expert_views(slot.t)
            names = (("L0_ffn_Wsu", "L0_ffn_Wsg", "L0_ffn_Wsd") if e == E_ROUTED else
                     ("L0_ffn_Wup", "L0_ffn_Wgate", "L0_ffn_Wdown"))
            srcs = [a[n] if e == E_ROUTED else a[n][e, :, :] for n in names]
            w_e_loaded[e] = (slot, load([(view[:, i, :, :], s.rearrange("(c p) n -> p c n", p=P))
                                         for i, s in enumerate(srcs)], slot.free))

        def split_expert(e):
            slot, w_load = w_e_loaded[e]
            dst = w_ring.next()
            views = Pair(expert_views(dst.t.hi), expert_views(dst.t.lo))
            tokens = []
            for i in range(3):
                tokens += split_sbuf(views[:, i, :, :], expert_views(slot.t)[:, i, :, :], w_load, dst.free)
            slot.free = tokens[-2:]
            w_e_ready[e] = (dst, views, tokens)
            if e + 2 < NE:
                load_expert(e + 2)
            elif e + 2 == NE:
                load_qkv()
            else:
                load_ffn(0)

        def load_experts_front():
            z = pool.add(lambda e: e.memset(w_router_in[:, :, :], 0.0))
            z2 = pool.add(lambda e: e.memset(router_rows[:, :, :], 0.0))
            wl = load([(w_router_in[:, :, 0:E_ROUTED], a["L0_ffn_Wr"].rearrange("(c p) n -> p c n", p=P)),
                       (router_rows[:, 0, 0:E_ROUTED], a["L0_ffn_br"].partition_broadcast(P)),
                       (router_rows[:, 1, 0:E_ROUTED], a["L0_ffn_gate_bias"].partition_broadcast(P)),
                       (iota[:, :], a["iota"]),
                       (b_down[0:E_ROUTED, :], a["L0_ffn_bdown"]), (b_down[E_ROUTED:NE, :], a["bsd_row"]),
                       (b_up[:, 0:E_ROUTED, :], a["bup_cols"]), (b_up[:, E_ROUTED, :], a["bsu_cols"]),
                       (b_gate[:, 0:E_ROUTED, :], a["bgate_cols"]), (b_gate[:, E_ROUTED, :], a["bsg_cols"])],
                      z, z2)
            ready["router"] = (wl, split_sbuf(Pair(w_router.hi[:, :, :], w_router.lo[:, :, :]),
                                              w_router_in[:, :, :], wl))
            yield

        def router(b):
            tiles = [TB * b + i for i in range(TB)]
            wl, w_w = need_inner("router")
            w_xT = need_inner(("xT_experts", b))
            rt = router_ring.next()
            gate, bias, pick, tmp = (rt.t[:, i, :, :] for i in range(4))
            idx, stat = rt_idx.next(), rt_stat.next()
            bank = trans.next()
            view = bank.t[:, 0:TB * NE].rearrange("p (t e) -> p t e", e=NE)
            for i, t in enumerate(tiles):
                w = mm(view[:, i, :], [(xT_pair[:, c, t * P:(t + 1) * P], w_router[:, c, :]) for c in range(DC)],
                       w_xT, w_w, bank.free, signal=i == TB - 1)
            rows = [router_rows[:, j, :].unsqueeze(1).to_broadcast([P, TB, NE]) for j in range(2)]
            w = tt(dve, gate, view, rows[0], ALU.add, w, wl, rt.free)
            bank.free = [w]
            w_gate = w
            w = tt(dve, bias, gate, rows[1], ALU.add, w)
            w = dve.add(lambda e: e.memset(bias[:, :, E_ROUTED:], -3.0e38), w)
            for i in range(TB):
                w8 = dve.add(lambda e, i=i: e.max(stat.t[:, i, :], bias[:, i, :]), w, stat.free)
                w_i = dve.add(lambda e, i=i: e.max_index(idx.t[:, i, :], stat.t[:, i, :], bias[:, i, :]), w8, idx.free)
            w = dve.add(lambda e: e.tensor_copy(stat.t[:, :, 0:2], idx.t[:, :, 0:2]), w_i)
            for i in range(TB):
                w1 = ts(dve, pick[:, i, :], iota[:, :], stat.t[:, i, 0:1], None, ALU.is_equal, None, w, wl)
                w2 = stt(dve, pick[:, i, :], iota[:, :], stat.t[:, i, 1:2], pick[:, i, :], ALU.is_equal, ALU.add, w1)
            yield
            w = ts(dve, tmp, pick, -NEG, NEG, ALU.mult, ALU.add, w2)
            w_m = tt(dve, tmp, tmp, gate, ALU.add, w, w_gate)
            w = dve.add(lambda e: e.reduce_max(stat.t[:, :, 2], tmp, mybir.AxisListType.X), w_m)
            w = tt(dve, tmp, tmp, stat.t[:, :, 2:3].to_broadcast([P, TB, NE]), ALU.subtract, w)
            w = act_op(tmp, tmp, ACT.Exp, w)
            w = dve.add(lambda e: e.reduce_sum(stat.t[:, :, 3], tmp, mybir.AxisListType.X), w)
            w = dve.add(lambda e: e.reciprocal(stat.t[:, :, 3], stat.t[:, :, 3]), w)
            rows_b = slice(TB * b, TB * b + TB)
            w = tt(dve, probs_e[:, rows_b, :], tmp, stat.t[:, :, 3:4].to_broadcast([P, TB, NE]), ALU.mult, w)
            w_p = dve.add(lambda e: e.memset(probs_e[:, rows_b, E_ROUTED:], 1.0), w)
            rt.free = idx.free = stat.free = [w_p]
            yield
            bank = trans.next()
            for i, t in enumerate(tiles):
                w = transpose(bank.t[0:NE, i * P:(i + 1) * P], probs_e[:, t, :], w_p, bank.free, signal=True)
            pe_T = probs_eT_ring.next()
            w_pT = dve.add(lambda e, bank=bank: e.tensor_copy(pe_T.t[:, :], bank.t[0:NE, 0:S]), w, pe_T.free)
            bank.free = [w_pT]
            yield
            bank = trans.next()
            for i, t in enumerate(tiles):
                w = mm(bank.t[:, i * D:(i + 1) * D], [(pe_T.t[:, i * P:(i + 1) * P], b_down[:, :])],
                       w_pT, wl, bank.free)
            w = tt(dve, y[:, rows_b, :], bank.t[:, :].rearrange("p (t d) -> p t d", d=D), x[:, rows_b, :],
                   ALU.add, w, need_inner(("x_experts", b)))
            bank.free = pe_T.free = [w]
            ready["router", b] = [w, w_p]
            yield

        acc_tokens = {}

        def expert(e, h):
            w_x = [w for b in range(TB * h, TB * h + 2) for w in need(("xT_experts", b))]
            w_slot, wp, w_w = w_e_ready[e]
            cols = slice(h * HALF, (h + 1) * HALF)
            u, up, sl, gp = u_ring.next(), u_pair.next(), s_ring.next(), g_pair.next()
            w_u, w_up = [], []
            for i in range(DC):
                bank = banks[i]
                w = mm(bank.t[:, :], [(wp[:, 0, c, i * P:(i + 1) * P], xT_pair[:, c, cols]) for c in range(DC)],
                       w_w, w_x, bank.free)
                bias = b_up[:, e, i:i + 1]
                w_u.append(act_op(u.t[:, i, :], bank.t[:, :], ACT.Identity, w, u.free, bias=bias))
                w_hi = act_op(up.t.hi[:, i, :], bank.t[:, :], ACT.Identity, w, up.free, bias=bias)
                w_lo = stt(dve, up.t.lo[:, i, :], bank.t[:, :], bias, plain(up.t.hi[:, i, :]), ALU.add, ALU.subtract,
                           w_hi, up.free)
                bank.free = [w_lo]
                w_up += [w_hi, w_lo]
            if e == NE - 1:
                for b in (2 * h, 2 * h + 1):
                    xT_free[b] = [w]
            yield
            w_g = []
            for j in range(DC):
                bank = banks[2 + j]
                w = mm(bank.t[:, :], [(wp[:, 1, c, j * P:(j + 1) * P], up.t[:, c, :]) for c in range(DC)],
                       w_up, bank.free)
                w_s = act_op(sl.t[:, j, :], bank.t[:, :], ACT.Silu, w, sl.free, bias=b_gate[:, e, j:j + 1])
                bank.free = [w_s]
                w_m = tt(pool, sl.t[:, j, :], sl.t[:, j, :], u.t[:, j, :], ALU.mult, w_s, w_u)
                w_hi = act_op(gp.t.hi[:, j, :], sl.t[:, j, :], ACT.Copy, w_m, gp.free)
                w_lo = tt(dve, gp.t.lo[:, j, :], sl.t[:, j, :], plain(gp.t.hi[:, j, :]), ALU.subtract, w_hi, gp.free)
                w_g += [w_hi, w_lo]
            up.free = [w]
            u.free, sl.free = [w_m], [w_lo]
            yield
            for i in range(TH // 2):
                bank = banks[6 + i]
                for j in range(2):
                    t = h * TH + 2 * i + j
                    w = mm(bank.t[:, j * D:(j + 1) * D],
                           [(gp.t[:, c, (2 * i + j) * P:(2 * i + j + 1) * P], wp[:, 2, c, :]) for c in range(DC)],
                           w_g, bank.free)
                for j in range(2):
                    t = h * TH + 2 * i + j
                    w_r = need(("router", t // TB))
                    w_acc = stt(dve, y[:, t, :], bank.t[:, j * D:(j + 1) * D], probs_e[:, t, e:e + 1],
                                y[:, t, :], ALU.mult, ALU.add, w, w_r, acc_tokens.get(t))
                    acc_tokens[t] = w_acc
                bank.free = [w_acc]
            gp.free = [w]
            if h == 1:
                w_slot.free = [w]
                if e + 2 < NE:
                    split_expert(e + 2)
                elif e + 2 == NE:
                    split_qkv()
            if e == NE - 1:
                for b in (2 * h, 2 * h + 1):
                    background.append(finish_experts(b))
            yield

        def finish_experts(b):
            tiles = [TB * b + i for i in range(TB)]
            w_x = layer_norm(y_tile, x_tile, tiles, [acc_tokens[t] for t in tiles])
            yield
            ready["xT_attn1", b] = transpose_x(b, w_x)
            ready["x_attn1", b] = w_x
            yield

        SCALE1 = float(HD1) ** -0.5

        def load_qkv():
            slot = raw_ring.next()
            raw = slot.t[:, 0:3 * DC * D].rearrange("p (c n) -> p c n", c=DC)
            ready["qkv_in"] = (slot, raw, load([(raw, a["L1_attn_Wqkv"].rearrange("(c p) n -> p c n", p=P))],
                                               slot.free))

        def split_qkv():
            slot, raw, wl = ready["qkv_in"]
            dst = w_ring.next()
            w_qkv = Pair(*(t[:, :].rearrange("p (c n) -> p c n", c=DC) for t in (dst.t.hi, dst.t.lo)))
            got = split_sbuf(w_qkv[:, :, :], raw, wl, dst.free)
            slot.free = got
            ready["w_qkv"] = (dst, w_qkv, got)
            load_ffn(1)

        def load_attn1(wait):
            z = pool.add(lambda e: e.memset(w_out1[:, :, :], 0.0), wait)
            src = a["L1_attn_Wout"].rearrange("(g j r) n -> j r g n", j=GH, r=HD1)
            return load([(b_qkv[:, :], a["L1_attn_bqkv"].partition_broadcast(P)),
                         (b_out1[:, :], a["L1_attn_bout"].partition_broadcast(P)),
                         (mask1[:, :, :], a["mask1"]), (rope1[:, :, :, :], a["rope1"]),
                         (row_mask[:, :], a["row_mask"]),
                         (ln_rows[:, 0, :], a["L1_xattn_ln_gamma"].partition_broadcast(P)),
                         (ln_rows[:, 1, :], a["L1_xattn_ln_beta"].partition_broadcast(P))]
                        + [(w_out1[j * HS1:j * HS1 + HD1, :, :], src[j]) for j in range(GH)], z, wait)

        qkv_ready = {}

        def project_qkv(b):
            w_slot, w_qkv, w_w = ready["w_qkv"]
            w_xT = need(("xT_attn1", b))
            qT, kT, v_tok = q1_ring.next(), k1_ring.next(), v_ring.next()
            tiles = [TB * b + i for i in range(TB)]
            v_bank = trans.next()
            toks, pbanks = [], []
            for i, t in enumerate(tiles):
                bank = proj.next()
                pbanks.append(bank)
                xt = [xT_pair[:, c, t * P:(t + 1) * P] for c in range(DC)]
                w = mm(bank.t[:, :], [(xt[c], w_qkv[:, c, 0:2 * D]) for c in range(DC)], w_w, w_xT, bank.free)
                qk, rp = qk_ring.next(), qk_rope.next()
                w_b = tt(dve, qk.t[:, :, :], bank.t[:, :].rearrange("p (h d) -> p h d", d=HD1),
                         b_qkv[:, 0:2 * D].rearrange("p (h d) -> p h d", d=HD1), ALU.add, w, qk.free, w_attn1_const)
                bank.free = [w_b]
                hd = HD1 // 2

                def row(j, lo_, hi_):
                    return rope1[:, i, j, lo_:hi_].unsqueeze(1).to_broadcast([P, 2 * H1, hi_ - lo_])

                w1 = tt(pool, rp.t[:, 0, :, :], qk.t[:, :, :], row(0, 0, HD1), ALU.mult, w_b, rp.free)
                tt(dve, rp.t[:, 1, :, 0:hd], qk.t[:, :, hd:HD1], row(1, 0, hd), ALU.mult, w_b, rp.free)
                w2 = tt(dve, rp.t[:, 1, :, hd:HD1], qk.t[:, :, 0:hd], row(1, hd, HD1), ALU.mult)
                w_q = tt(dve, qk.t[:, :, :], rp.t[:, 0, :, :], rp.t[:, 1, :, :], ALU.add, w1, w2)
                rp.free = [w_q]
                toks.append((qk, w_q))
                wv_ = mm(v_bank.t[:, i * D:(i + 1) * D], [(xt[c], w_qkv[:, c, 2 * D:]) for c in range(DC)],
                         v_bank.free)
            xT_free[b] = [wv_]
            for i, t in enumerate(tiles):
                w_v = tt(dve, v_tok.t[:, i, :, 0:HD1], v_bank.t[:, i * D:(i + 1) * D].rearrange("p (h d) -> p h d", d=HD1),
                         b_qkv[:, 2 * D:].rearrange("p (h d) -> p h d", d=HD1), ALU.add, wv_, v_tok.free, zv)
            v_bank.free = [w_v]
            yield
            got = []
            for i, (qk, w_q) in enumerate(toks):
                bank = pbanks[i]
                flat = qk.t[:, :, :].rearrange("p h d -> p (h d)")
                for j in range(4):
                    w = transpose(bank.t[:, j * P:(j + 1) * P], flat[:, j * P:(j + 1) * P], w_q, bank.free,
                                  signal=j == 3)
                qk.free = [w]
                w_k = act_op(kT.t[:, :, i * P:(i + 1) * P], bank.t[:, 2 * P:].rearrange("p (g s) -> p g s", s=P),
                             ACT.Copy, w, kT.free)
                w_q = act_op(qT.t[:, :, i * P:(i + 1) * P], bank.t[:, 0:2 * P].rearrange("p (g s) -> p g s", s=P),
                             ACT.Copy, w, qT.free)
                bank.free = [w_q]
                got += [w_k, w_q]
            if b == B - 1:
                w_slot.free = [wv_]
                split_ffn(1)
            qkv_ready[b] = (qT, kT, v_tok, got + [w_v])
            yield

        def attention1_group(b, g):
            qT, kT, v_tok, w_qkv_done = qkv_ready[b]
            qm = q1m_ring.next()
            first = g * GH % NP8
            w_qm = tt(pool, qm.t[:, :, :], qT.t[:, g * GH // NP8, :].unsqueeze(1).to_broadcast([P, GH, S]),
                      row_mask[:, first:first + GH].unsqueeze(2).to_broadcast([P, GH, S]), ALU.mult,
                      w_qkv_done, qm.free)
            fronts, probs = [], []
            yield
            for h in range(g * GH, (g + 1) * GH):
                bank = score.next()
                for i in range(TB):
                    w = mm(bank.t[:, i * S:(i + 1) * S], [(qm.t[:, h % GH, i * P:(i + 1) * P], kT.t[:, h // NP8, :])],
                           w_qm, w_qkv_done, bank.free)
                fronts.append(exponentials(bank, w, [(slice(i * S, (i + 1) * S), mask1[:, i, :]) for i in range(TB)],
                                           SCALE1))
                if h % GH == 1:
                    yield
            qm.free = [w]
            if g == G1 - 1:
                qT.free, kT.free = [w_qm], [w]
            probs += [normalised(f) for f in fronts[:2]]
            yield
            probs += [normalised(f) for f in fronts[2:]]
            pTs = []
            for h, (p, w_p) in enumerate(probs):
                bank, pT = trans.next(), pT_ring.next()
                for j in range(TB):
                    for i in range(TB):
                        w = transpose(bank.t[:, j * S + i * P:j * S + (i + 1) * P],
                                      p.t[:, i * S + j * P:i * S + (j + 1) * P], w_p, bank.free,
                                      signal=i == j == TB - 1)
                p.free = [w]
                if h % 2:
                    w = dve.add(lambda e, pT=pT, bank=bank: e.tensor_copy(pT.t[:, :], bank.t[:, :]), w, pT.free)
                else:
                    w = act_op(pT.t[:, :], bank.t[:, :], ACT.Copy, w, pT.free)
                bank.free = [w]
                pTs.append((pT, w))
                if h == 1:
                    yield
            yield
            bank = pv_bank
            for h, (pT, w_pT) in enumerate(pTs):
                w = mm(bank.t[h * HS1:(h + 1) * HS1, 0:S],
                       [(v_tok.t[:, j, g * GH + h, :], pT.t[:, j * S:(j + 1) * S]) for j in range(TB)],
                       w_pT, bank.free, shared=True)
                pT.free = [w]
            if g == G1 - 1:
                v_tok.free = [w]
            c1 = ctx1_ring.next()
            w_c = act_op(c1.t[:, :], bank.t[:, 0:S], ACT.Copy, w, c1.free)
            bank.free = [w_c]
            yield
            for i in range(TB):
                w = mm(acc_bank.t[:, i * D:(i + 1) * D], [(c1.t[:, i * P:(i + 1) * P], w_out1[:, g, :])],
                       w_c, acc_bank.free if g == 0 else None, start=g == 0 and i == 0, stop=g == G1 - 1, shared=True)
            c1.free = [w]
            if g == G1 - 1:
                rows = slice(TB * b, TB * b + TB)
                w1 = tt(dve, y[:, rows, :], acc_bank.t[:, :].rearrange("p (t d) -> p t d", d=D), x[:, rows, :],
                        ALU.add, w, need_inner(("x_attn1", b)))
                acc_bank.free = [w1]
                w1 = tt(dve, y[:, rows, :], y[:, rows, :], b_out1[:, :].unsqueeze(1).to_broadcast([P, TB, D]),
                        ALU.add, w1)
                background.append(bilinear(b, w1))
            yield

        def bilinear(b, w_y):
            tiles = [TB * b + i for i in range(TB)]
            w_x = layer_norm(y_tile, x_tile, tiles, w_y)
            yield
            w_xT = transpose_x(b, w_x, dst=xT)
            yield
            w_k = need_inner("context_keys")
            o, s, st = outT_ring.next(), bi_ring.next(), bi_stat.next()
            bank = trans.next()
            w = mm(bank.t[0:CTX, 0:S], [(kv_tok[:, tiles[c], :], xT[:, c, b * S:(b + 1) * S]) for c in range(DC)],
                   w_xT, w_k, bank.free)
            w_o = act_op(o.t[:, :], bank.t[0:CTX, 0:S], ACT.Copy, w, o.free)
            bank.free = [w_o]
            yield
            bank = trans.next()
            for i in range(TB):
                w = mm(bank.t[:, i * S:(i + 1) * S], [(o.t[:, i * P:(i + 1) * P], kvT[:, b * S:(b + 1) * S])],
                       w_o, w_k, bank.free)
            o.free = [w]
            w = act_op(s.t[:, :, :], bank.t[:, :].rearrange("p (t d) -> p t d", d=S), ACT.Copy, w, s.free,
                       scale=float(D) ** -0.5)
            bank.free = [w]
            yield

            def s_tile(t):
                return s.t[:, t - tiles[0], :]

            w_n = layer_norm(s_tile, s_tile, tiles, w, eps=1e-6)
            yield
            rows = [ln_rows[:, j, :].unsqueeze(1).to_broadcast([P, TB, S]) for j in range(2)]
            w = tt(dve, s.t[:, :, :], s.t[:, :, :], rows[0], ALU.mult, w_n, w_attn1_const)
            w = tt(dve, s.t[:, :, :], s.t[:, :, :], rows[1], ALU.add, w)
            w = dve.add(lambda e: e.reduce_max(st.t[:, 0, :], s.t[:, :, :], mybir.AxisListType.X), w, st.free)
            w = ts(dve, st.t[:, 0, :], st.t[:, 0, :], -1.0, None, ALU.mult, None, w)
            for i in range(TB):
                w_e = act_op(s.t[:, i, :], s.t[:, i, :], ACT.Exp, w, bias=st.t[:, 0, i:i + 1],
                             accum_out=st.t[:, 1, i:i + 1])
            w = dve.add(lambda e: e.reciprocal(st.t[:, 2, :], st.t[:, 1, :]), w_e)
            w_m = []
            for i, t in enumerate(tiles):
                w_m.append(stt(dve, y[:, t, :], s.t[:, i, :], st.t[:, 2, i:i + 1], x[:, t, :], ALU.mult, ALU.add, w))
            s.free = st.free = w_m[-1:]
            yield
            w_x = layer_norm(y_tile, x_tile, tiles, w_m)
            yield
            ready["xT_ffn", b] = transpose_x(b, w_x)
            ready["x_ffn", b] = w_x
            yield

        ffn_raw, ffn_ready = {}, {}
        MT = 2

        def ffn_views(t):
            n = 2 * DC * MT * P
            return (t[:, 0:n].rearrange("p (i c n) -> p i c n", i=2, c=DC),
                    t[:, n:n + MT * D].rearrange("p (m n) -> p m n", n=D))

        def load_ffn(u):
            slot = raw_ring.next()
            gu, dn = ffn_views(slot.t)
            m = u % (HT // MT) * MT
            cols = slice(m * P, (m + MT) * P)
            ffn_raw[u] = (slot, load([(gu[:, i, :, :], a[name].rearrange("(c p) n -> p c n", p=P)[:, :, cols])
                                      for i, name in enumerate(("w_gateT", "w_upT"))]
                                     + [(dn, a["w_downT"].rearrange("(m p) n -> p m n", p=P)[:, m:m + MT, :])],
                                     slot.free))

        NU = NHALF * HT // MT

        def split_ffn(u):
            slot, wl = ffn_raw[u]
            dst = w_ring.next()
            (gu_hi, dn_hi), (gu_lo, dn_lo) = ffn_views(dst.t.hi), ffn_views(dst.t.lo)
            gu, dn = ffn_views(slot.t)
            got = []
            for i in range(2):
                got += split_sbuf(Pair(gu_hi[:, i, :, :], gu_lo[:, i, :, :]), gu[:, i, :, :], wl, dst.free)
            got += split_sbuf(Pair(dn_hi, dn_lo), dn, wl, dst.free)
            slot.free = got[-2:]
            ffn_ready[u] = (dst, Pair(gu_hi, gu_lo), Pair(dn_hi, dn_lo), got)
            if u + 2 < NU:
                load_ffn(u + 2)

        def ffn(h, m):
            u = h * (HT // MT) + m // MT
            w_slot, w_gu, w_dn, w_w = ffn_ready[u]
            w_x = [w for b in range(2 * h, 2 * h + 2) for w in need(("xT_ffn", b))]
            cols = slice(h * HALF, (h + 1) * HALF)
            rows = slice(m % MT * P, (m % MT + 1) * P)
            got = []
            for i in range(2):
                bank = banks[2 * (m % 2) + i]
                got.append((bank, mm(bank.t[:, :], [(w_gu[:, i, c, rows], xT_pair[:, c, cols]) for c in range(DC)],
                                     w_w, w_x, bank.free)))
            (gate, w_gate), (up, w_up) = got
            sl, gp = p_ring.next(), g1_pair.next()
            w_s = act_op(sl.t[:, :], gate.t[:, :], ACT.Silu, w_gate, sl.free)
            gate.free = [w_s]
            w_m = tt(dve, sl.t[:, :], up.t[:, :], sl.t[:, :], ALU.mult, w_s, w_up)
            up.free = [w_m]
            w_hi = act_op(gp.t.hi[:, :], sl.t[:, :], ACT.Copy, w_m, gp.free)
            w_lo = tt(dve, gp.t.lo[:, :], sl.t[:, :], plain(gp.t.hi[:, :]), ALU.subtract, w_hi, gp.free)
            sl.free = [w_lo, w_hi]
            yield
            yield
            for i in range(TH):
                bank = banks[6 + i // 2]
                w = mm(bank.t[:, (i % 2) * D:(i % 2 + 1) * D],
                       [(gp.t[:, i * P:(i + 1) * P], w_dn[:, m % MT, :])], w_hi, w_lo,
                       bank.free if m == 0 else None, start=m == 0 and i % 2 == 0, stop=m == HT - 1, shared=True)
            gp.free = [w]
            if m % MT == MT - 1:
                w_slot.free = [w]
                if u + 2 < NU:
                    split_ffn(u + 2)
            if m == HT - 1:
                for i in range(2):
                    bank, b = banks[6 + i], 2 * h + i
                    rows_b = slice(TB * b, TB * b + TB)
                    w_y = tt(dve, y[:, rows_b, :], bank.t[:, :].rearrange("p (t d) -> p t d", d=D), x[:, rows_b, :],
                             ALU.add, w, ready["x_ffn", b])
                    bank.free = [w_y]
                    tiles = [TB * b + j for j in range(TB)]
                    w_x = layer_norm(y_tile, x_tile, tiles, w_y)
                    store(b, w_x)
            yield

        stores = []

        def store(b, w_x):
            done = sem(f"store{b}")
            sp.add(lambda e: e.dma_start(out_dram[b].rearrange("(t p) d -> p t d", p=P),
                                         x[:, TB * b:TB * b + TB, :]).then_inc(done, 16), w_x, signal=False)
            stores.append((done, 16))

        background.append(learned_adjacency())
        background.append(context_keys())
        units = []
        for g in range(NG):
            for b in range(B):
                if b == B - 1 and g + 1 < NG:
                    units.append((prepare_group_weights(g + 1), 0))
                units.append((attention_group(b, g), 2))
        pipeline(units, 1)
        while "adjacency_done" not in ready:
            advance()

        stage_read = [last(q) for q in (pe, act, dve, pool)]
        memory0.close()
        stage_memory()
        b_qkv = sb("b_qkv", [P, 3 * D])
        w_out1 = sb("w_out1", [P, G1, D])
        b_out1 = sb("b_out1", [P, D])
        ln_rows = sb("ln_rows", [P, 2, S])
        mask1 = sb("mask1", [P, TB, S])
        rope1 = sb("rope1", [P, TB, 2, HD1])
        row_mask = sb("row_mask", [P, P // HD1])
        w_attn1_const = load_attn1(stage_read)
        memory1 = stage_memory()
        u_ring = ring("u", 2, [P, DC, HALF])
        s_ring = ring("silu", 2, [P, DC, HALF])
        u_pair = pair_ring("u_pair", 2, [P, DC, HALF])
        g_pair = pair_ring("g_pair", 2, [P, DC, HALF])
        for r in (u_ring, s_ring, u_pair, g_pair):
            for slot in r.slots:
                slot.free = list(stage_read)
        split_expert(0)
        split_expert(1)
        order = [(0, 0), (1, 0), (0, 1), (1, 1)] + [(e, h) for e in range(2, NE) for h in range(NHALF)]
        pipeline([(expert(e, h), 1) for e, h in order], 2)
        stage_read = [last(q) for q in (pe, act, dve, pool)]
        memory1.close()
        stage_memory()
        NP8 = P // HD1
        v_ring = ring("v_tok", 2, [P, TB, H1, HS1])
        qk_ring = ring("qk_tok", 2, [P, 2 * H1, HD1])
        qk_rope = ring("qk_rope", 2, [P, 2, 2 * H1, HD1])
        q1_ring = ring("qT1", 2, [P, H1 // NP8, S])
        k1_ring = ring("kT1", 2, [P, H1 // NP8, S])
        q1m_ring = ring("q_masked", 2, [P, GH, S])
        ctx1_ring = ring("ctx1", 2, [P, S])
        bi_ring = ring("bilinear", 2, [P, TB, S])
        bi_stat = ring("bi_stat", 2, [P, 3, TB])
        outT_ring = ring("outT", 2, [CTX, S])
        g1_pair = pair_ring("g1_pair", 3, [P, HALF])
        for r in (v_ring, qk_ring, qk_rope, q1_ring, k1_ring, q1m_ring, ctx1_ring, bi_ring, bi_stat, outT_ring,
                  g1_pair):
            for slot in r.slots:
                slot.free = list(stage_read)
        zv = [pool.add(lambda e, v=v: e.memset(v.t[:, :, :, :], 0.0), v.free) for v in v_ring.slots]
        units = [(project_qkv(0), 1)]
        for b in range(B):
            for g in range(G1):
                if g == 2 and b + 1 < B:
                    units.append((project_qkv(b + 1), 0))
                units.append((attention1_group(b, g), 2))
        split_ffn(0)
        pipeline(units, 1)
        pipeline([(ffn(h, m), 1) for h in range(NHALF) for m in range(HT)])
        assert not background
        for w in stores:
            sp.add(None, w, signal=False)

        block = ctx.enter_context(nc.Block())

        @block.sync
        def _(e):
            sp.play(e)

        @block.tensor
        def _(e):
            pe.play(e)

        @block.scalar
        def _(e):
            act.play(e)

        @block.vector
        def _(e):
            dve.play(e)

        @block.gpsimd
        def _(e):
            pool.play(e)


def rope_table(n, dim):
    inv = (1.0 / np.float32(10000.0) ** (np.arange(0, dim, 2, dtype=np.float32) / np.float32(dim))).astype(np.float32)
    angle = np.arange(n, dtype=np.float32)[:, None] * inv
    cos, sin = np.cos(angle).astype(np.float32), np.sin(angle).astype(np.float32)
    return np.stack([np.concatenate([cos, cos], 1), np.concatenate([-sin, sin], 1)], 1)


def constants():
    q, k = np.arange(P)[:, None], np.arange(S)[None, :]
    mask0 = np.where(k - P > q, np.float32(NEG), np.float32(0))
    rows = np.arange(S).reshape(TB, P).T
    mask1 = np.where(np.arange(S)[None, None, :] > rows[:, :, None], np.float32(-10000.0 * HD1 ** 0.5), np.float32(0))

    def by_tile(t):
        return np.ascontiguousarray(t.reshape(TB, P, *t.shape[1:]).swapaxes(0, 1))

    return {
        "identity": np.eye(P, dtype=np.float32),
        "mask0": mask0.astype(np.float32),
        "mask1": mask1.astype(np.float32),
        "rope0": by_tile(rope_table(S, DR)),
        "rope1": by_tile(rope_table(S, HD1)),
        "row_mask": (np.arange(P)[:, None] // HD1 == np.arange(P // HD1)[None, :]).astype(np.float32),
        "iota": np.broadcast_to(np.arange(NE, dtype=np.float32), (P, NE)).copy(),
    }


def layouts(w):
    q_b = w["L0_attn_q_b_w"].reshape(QLR, NH, DQK)
    kv_b = w["L0_attn_kv_b_w"].reshape(KVLR, NH, DN + DV)
    out = {
        "x": w["x"],
        "xT": w["x"].reshape(T, D).T,
        "ctxT": w["ctx_512"].reshape(T, CTX).T,
        "w_nopeT": q_b[:, :, :DN].transpose(2, 1, 0),
        "w_rot": q_b[:, :, DN:],
        "w_k_latT": kv_b[:, :, :DN].transpose(2, 1, 0),
        "w_v_latT": kv_b[:, :, DN:].transpose(2, 1, 0),
        "w_o": w["L0_attn_o_w"].reshape(NH, DV, D).transpose(1, 0, 2),
        "q_ln": w["L0_attn_q_a_ln_w"].reshape(2, KQ).T,
        "L0_xattn_WqT": w["L0_xattn_Wq"].T,
        "L0_xattn_WkT": w["L0_xattn_Wk"].T,
        "gamma_raw": w["L0_xattn_gamma_raw"].reshape(1),
        "L1_xattn_WkT": w["L1_xattn_W_k"].T,
        "L1_b_col": w["L1_xattn_b_k"].reshape(CTX, 1),
        "bsd_row": w["L0_ffn_bsd"].reshape(1, D),
        "bup_cols": w["L0_ffn_bup"].reshape(E_ROUTED, DC, P).transpose(2, 0, 1),
        "bsu_cols": w["L0_ffn_bsu"].reshape(DC, P).T,
        "bgate_cols": w["L0_ffn_bgate"].reshape(E_ROUTED, DC, P).transpose(2, 0, 1),
        "bsg_cols": w["L0_ffn_bsg"].reshape(DC, P).T,
        "w_gateT": w["L1_ffn_w_gate"].T,
        "w_upT": w["L1_ffn_w_up"].T,
        "w_downT": w["L1_ffn_w_down"].T,
    }
    for name in ("L0_attn_q_a_w", "L0_attn_kv_a_w", "L0_attn_kv_a_ln_w", "L0_ffn_Wr", "L0_ffn_br", "L0_ffn_gate_bias",
                 "L0_ffn_Wup", "L0_ffn_Wgate", "L0_ffn_Wdown", "L0_ffn_bdown", "L0_ffn_Wsu", "L0_ffn_Wsg", "L0_ffn_Wsd",
                 "L1_attn_Wqkv", "L1_attn_bqkv", "L1_attn_Wout", "L1_attn_bout", "L1_xattn_b_k", "L1_xattn_ln_gamma",
                 "L1_xattn_ln_beta"):
        out[name] = w[name]
    return out


def kernel(**inputs):
    from concourse import bacc
    from concourse.bass_utils import run_bass_kernel_spmd

    arrays = layouts({k: np.asarray(v) for k, v in inputs.items()})
    arrays.update(constants())
    arrays = {k: np.ascontiguousarray(v) for k, v in arrays.items()}
    nc = bacc.Bacc("TRN2", target_bir_lowering=False, num_devices=1)
    aps = {k: nc.dram_tensor("in_" + k, v.shape, mybir.dt.from_np(v.dtype), kind="ExternalInput").ap()
           for k, v in arrays.items()}
    out = nc.dram_tensor("out", (B, S, D), F32, kind="ExternalOutput").ap()
    build(nc, aps, out)
    r = run_bass_kernel_spmd(nc, [{"in_" + k: v for k, v in arrays.items()}], core_ids=[0])
    return r.results[0]["out"]
```

```python
from contextlib import ExitStack

import numpy as np

import concourse.bass as bass
from concourse import mybir

F32 = mybir.dt.float32
F32R = mybir.dt.float32r
U32 = mybir.dt.uint32
I32 = mybir.dt.int32
ALU = mybir.AluOpType
ACT = mybir.ActivationFunctionType

P = 128
B, S, D = 4, 256, 256
T = B * S
NT = T // P
TB = S // P
DC = D // P
HALF = 512
NHALF = T // HALF
TH = HALF // P
CTX = 64

NH, QLR, KVLR, DR, DN, DV = 32, 192, 64, 64, 128, 128
QREST = QLR - P
DQK = DN + DR
GH = 4
NG = NH // GH
NEG = -1.0e30

TOPK = int(S * 0.3)
E_ROUTED = 7
NE = E_ROUTED + 1

H1, HD1 = 16, 16
HS1 = 32
HEADS_PER_TILE = P // HD1
G1 = H1 // GH
HID = 1024
HT = HID // P
LN_EPS = 1e-5


class Queue:

    def __init__(self, sem):
        self.sem, self.count, self.todo, self.seen = sem, 0, [], {}

    def add(self, fn, *waits, signal=True):
        need = {}
        stack = list(waits)
        while stack:
            w = stack.pop()
            if w is None:
                continue
            if isinstance(w, list):
                stack.extend(w)
                continue
            sem, value = w
            if self.seen.get(id(sem), 0) < value:
                need[id(sem)] = (sem, max(value, need.get(id(sem), (sem, 0))[1]))
        for key, (sem, value) in need.items():
            self.seen[key] = value
        self.count += signal
        self.todo.append((list(need.values()), fn, signal))
        return (self.sem, self.count) if signal else None

    def play(self, eng):
        for waits, fn, signal in self.todo:
            for sem, value in waits:
                eng.wait_ge(sem, value)
            ins = fn(eng) if fn else None
            if signal:
                ins.then_inc(self.sem, 1)


class Slot:

    def __init__(self, t):
        self.t, self.free, self.taken = t, [], False

    def __setattr__(self, name, value):
        object.__setattr__(self, name, value)
        if name == "free":
            object.__setattr__(self, "taken", False)


class Ring:
    def __init__(self, slots):
        self.slots, self.at = slots, 0

    def next(self):
        s = self.slots[self.at % len(self.slots)]
        assert not s.taken, "its last user has not said when it is free"
        s.taken = True
        self.at += 1
        return s


class Pair:

    def __init__(self, hi, lo):
        self.hi, self.lo = hi, lo

    def __getitem__(self, key):
        return Pair(self.hi[key], self.lo[key])


def plain(ap):
    return ap.bitcast(F32)


def build(nc, a, out_dram):
    with ExitStack() as ctx:
        scope = [(ctx, "left")]

        def sb(name, shape, dt=F32):
            stack, side = scope[0]
            return stack.enter_context(nc.sbuf_tensor(name, shape, dt, side=side))

        def stage_memory(side="left"):
            stack = ctx.enter_context(ExitStack())
            scope[0] = (stack, side)
            return stack

        def last_so_far():
            return [(q.sem, q.count) for q in (pe, act, dve, pool)]

        def sem(name):
            return ctx.enter_context(nc.semaphore(name))

        def ring(name, n, shape, dt=F32):
            return Ring([Slot(sb(f"{name}{i}", shape, dt)) for i in range(n)])

        def pair(name, shape):
            return Pair(sb(name + "_hi", shape, F32R), sb(name + "_lo", shape, F32R))

        def pair_ring(name, n, shape):
            return Ring([Slot(pair(f"{name}{i}", shape)) for i in range(n)])

        pe, act, dve, pool, sp = (Queue(sem(n)) for n in ("pe_done", "act_done", "dve_done", "pool_done", "sp_done"))
        banks = [Slot(ctx.enter_context(nc.psum_tensor(f"bank{i}", [P, 512], F32))) for i in range(8)]

        loads = [0]

        def load(pairs, *waits):
            done = sem(f"load{loads[0]}")
            loads[0] += 1
            for n, (dst, src) in enumerate(pairs):
                sp.add(lambda e, dst=dst, src=src: e.dma_start(dst, src).then_inc(done, 16),
                       *(waits if n == 0 else ()), signal=False)
            return (done, 16 * len(pairs))

        def mm(out, terms, *waits, start=True, stop=True, shared=False, signal=True):
            passes = []
            for lhsT, rhs in terms:
                if isinstance(lhsT, Pair):
                    passes += [(lhsT.hi, rhs.hi), (lhsT.hi, rhs.lo), (lhsT.lo, rhs.hi)]
                else:
                    passes.append((lhsT, rhs))
            for n, (lhsT, rhs) in enumerate(passes):
                first, last = n == 0, n == len(passes) - 1
                token = pe.add(
                    lambda e, lhsT=lhsT, rhs=rhs, s=start and first, z=stop and last: nc.tensor.matmul(
                        out, lhsT, rhs, start=s, stop=z, skip_group_check=shared),
                    *(waits if first else ()), signal=signal and last)
            return token

        def transpose(out, in_, *waits, signal=False):
            rows = in_.shape[0]
            return pe.add(lambda e: nc.tensor.transpose(out, in_, ident[0:rows, 0:rows]), *waits, signal=signal)

        def act_op(out, in_, func, *waits, **kw):
            return act.add(lambda e: e.activation(out, in_, func, **kw), *waits)

        def ts(q, out, in0, s1, s2, op0, op1, *waits):
            if op1 is None:
                return q.add(lambda e: e.tensor_scalar(out, in0, s1, None, op0), *waits)
            return q.add(lambda e: e.tensor_scalar(out, in0, s1, s2, op0, op1), *waits)

        def tt(q, out, in0, in1, op, *waits):
            return q.add(lambda e: e.tensor_tensor(out, in0, in1, op), *waits)

        def stt(q, out, in0, s, in1, op0, op1, *waits):
            return q.add(lambda e: e.scalar_tensor_tensor(out=out, in0=in0, scalar=s, in1=in1, op0=op0, op1=op1),
                         *waits)

        def split_psum(dst, src, *waits):
            hi = act_op(dst.hi, src, ACT.Copy, *waits)
            lo = tt(dve, dst.lo, src, plain(dst.hi), ALU.subtract, hi, *waits)
            return [hi, lo]

        def split_sbuf(dst, src, *waits):
            hi = act_op(dst.hi, src, ACT.Copy, *waits)
            lo = tt(pool, dst.lo, src, plain(dst.hi), ALU.subtract, hi, *waits)
            return [hi, lo]

        def split_query_weights(q, dst, src, *waits):
            hi = act_op(dst.hi, src, ACT.Copy, *waits)
            lo = tt(q, dst.lo[:, 0, :, :], src[:, 0, :, :], plain(dst.hi[:, 0, :, :]), ALU.subtract, hi, *waits)
            twice = dst.hi[QREST:, 1, :, :]
            rest = tt(dve, twice, src[QREST:, 1, :, :], plain(twice), ALU.subtract, hi, *waits)
            return [hi, lo, rest]

        background, ready = [], {}

        def advance():
            for task in list(background):
                try:
                    next(task)
                except StopIteration:
                    background.remove(task)

        def given(key):
            return ready[key]

        def need(key):
            while key not in ready:
                assert background, key
                advance()
            return ready[key]

        def pipeline(tasks):
            running, wait = [], 0
            tasks = list(tasks)
            while tasks or running:
                while tasks and wait <= 0:
                    task, period = tasks.pop(0)
                    running.append(task)
                    wait = period
                    if period:
                        break
                wait -= 1
                for task in list(running):
                    try:
                        next(task)
                    except StopIteration:
                        running.remove(task)
                advance()

        ident = sb("identity", [P, P])
        iota = sb("iota", [P, NE])

        x = sb("x", [P, NT, D])
        y = sb("y", [P, NT, D])
        xT = sb("xT_plain", [P, DC, T])
        xT_pair = pair("xT", [P, DC, T])
        qaT = xT_pair
        ctxT = sb("ctxT", [CTX, T])
        adjacency = sb("adjacency", [P, NT, D])
        kv_tok = sb("kv_tok", [P, NT, CTX])
        kvT = sb("kvT", [CTX, T])
        p_ring = ring("probs", 8, [P, 2 * S])
        pT_ring = ring("probsT", 6, [P, 2 * S])
        soft_ring = ring("soft", 14, [P, 3, 2])
        RAW, SPLIT = GH * (QLR + 2 * KVLR + D) + 2 * GH * DR, 3 * DC * D
        raw_ring = ring("w_raw", 2, [P, RAW])
        w_ring = pair_ring("w_split", 2, [P, SPLIT])
        gate_col = sb("gate_col", [P, 4])
        w_router = pair("w_router", [P, DC, NE])
        w_router_in = sb("w_router_in", [P, DC, NE])
        router_rows = sb("router_rows", [P, 2, NE])
        b_down = sb("b_down", [NE, D])
        b_up = sb("b_up", [P, NE, DC])
        b_gate = sb("b_gate", [P, NE, DC])
        router_ring = ring("router_buf", 3, [P, 4, TB, NE])
        rt_idx = ring("rt_idx", 3, [P, TB, NE], U32)
        rt_stat = ring("rt_stat", 3, [P, TB, NE])
        probs_e = sb("probs_e", [P, NT, NE])
        probs_eT_ring = ring("probs_eT", 2, [NE, S])
        stat_ring = ring("stat", 5, [P, 3, 2 * NT])
        bn_ring = ring("bn", 3, [P, NT, 8])

        b_qkv = sb("b_qkv", [P, 3 * D])
        w_out1 = sb("w_out1", [P, G1, D])
        b_out1 = sb("b_out1", [P, D])
        ln_rows = sb("ln_rows", [P, 2, S])
        mask1 = sb("mask1", [P, TB, S])
        rope1 = sb("rope1", [P, TB, 2, HD1])
        row_mask = sb("row_mask", [P, HEADS_PER_TILE])

        proj = Ring(banks[0:2])
        score = Ring(banks[2:4])
        trans = Ring(banks[4:6])
        front = Ring(banks[0:4])
        pv_bank, acc_bank = banks[6], banks[7]

        memory_heads0 = stage_memory()
        key_tok = sb("key_tok", [P, NT, KVLR + DR])
        ctx_pair_ring = pair_ring("ctx_pair", 2, [P, 2, S])
        memory0 = stage_memory()
        mask0 = sb("mask0", [P, S])
        rope0 = sb("rope0", [P, TB, 2, DR])
        keyT = sb("keyT", [P, T])
        qk_x = sb("qk_x", [CTX, 2, T])
        sim_ring = ring("sim", 2, [P, 3, S])
        best_ring = ring("best", 2, [P, 8])
        w_qk_x = sb("w_qk_x", [CTX, 2, CTX])
        w_kv_x = sb("w_kv_x", [CTX, CTX])
        kv_bias_col = sb("kv_bias_col", [CTX, 1])
        kv_bias_row = sb("kv_bias_row", [P, CTX])
        memory_front = stage_memory()
        Q0 = KVLR + DR
        w_down0 = sb("w_down0", [P, DC, KVLR + DR + QLR])
        q_ln = sb("q_ln", [P, 2])
        kv_ln = sb("kv_ln", [P, KVLR])
        low = sb("low", [P, NT, Q0 + QLR + QREST])
        sums = sb("sums", [P, NHALF, 2, TH])
        square = sb("square", [P, 2, QLR])
        rope_tmp = sb("rope_tmp", [P, 2, NT, DR])

        l_xT = load([(xT[:, :, :], a["xT"].rearrange("(c p) t -> p c t", p=P))])
        l_low = load([(w_down0[:, :, Q0:], a["L0_attn_q_a_w"].rearrange("(c p) n -> p c n", p=P)),
                      (w_down0[:, :, 0:Q0], a["L0_attn_kv_a_w"].rearrange("(c p) n -> p c n", p=P))])
        raw0 = {}

        def raw_views(slot):
            t = slot.t
            cuts = np.cumsum([0, GH * QLR, GH * KVLR, 2 * GH * DR, GH * KVLR, GH * D])
            nope, k_lat, rot, v_lat, o = (slice(int(m), int(n)) for m, n in zip(cuts[:-1], cuts[1:]))
            return (t[:, nope].rearrange("p (h q) -> p h q", h=GH), t[:, k_lat].rearrange("p (h d) -> p h d", h=GH),
                    t[:, rot].rearrange("p (c h d) -> p c h d", c=2, h=GH),
                    t[:, v_lat].rearrange("p (h d) -> p h d", h=GH), t[:, o].rearrange("p (h n) -> p h n", h=GH))

        def load_group_weights(g):
            slot = raw_ring.next()
            nope, k_lat, rot, v_lat, o = raw_views(slot)
            h = slice(g * GH, (g + 1) * GH)
            w_q_in = load([(nope, a["w_nopeT"][:, h, :]), (k_lat, a["w_k_latT"][:, h, :])]
                          + [(rot[:, 0, :, :], a["w_rot"][0:P, h, :])]
                          + [(rot[at:at + QREST, 1, :, :], a["w_rot"][P:QLR, h, :]) for at in (0, QREST)], slot.free)
            w_v_in = load([(v_lat, a["w_v_latT"][:, h, :]), (o, a["w_o"][:, h, :])])
            raw0[g] = (slot, w_q_in, w_v_in)

        l_const = load([(mask0[:, :], a["mask0"]),
                        (rope0[:, :, :, :], a["rope0"]), (q_ln[:, :], a["q_ln"]),
                        (kv_ln[:, :], a["L0_attn_kv_a_ln_w"].partition_broadcast(P))])
        load_group_weights(0)
        l_ident = load([(ident[:, :], a["identity"])])
        l_x = load([(x[:, :, :], a["x"].rearrange("b (t p) d -> p (b t) d", p=P))])
        l_ctx = load([(ctxT[:, :], a["ctxT"])])
        l_x0 = load([(w_qk_x[:, 0, :], a["L0_xattn_WqT"]), (w_qk_x[:, 1, :], a["L0_xattn_WkT"]),
                     (gate_col[:, 0:1], a["gamma_raw"].partition_broadcast(P)),
                     (w_kv_x[:, :], a["L1_xattn_WkT"]), (kv_bias_col[:, :], a["L1_b_col"]),
                     (kv_bias_row[:, :], a["L1_xattn_b_k"].partition_broadcast(P))])
        load_group_weights(1)
        RSQRT_SEED, NEWTON_STEPS = float(0x5F3759DF), 3

        def rsqrt(v, n, eps, *waits, q=None):
            slot = stat_ring.next()
            ve, r, s = (slot.t[:, i, 0:n] for i in range(3))
            w_v = ts(dve, ve, v, eps, None, ALU.add, None, slot.free, *waits)
            w = ts(dve, r.bitcast(I32), ve.bitcast(I32), 1, None, ALU.logical_shift_right, None, w_v)
            w = ts(dve, r.bitcast(I32), r.bitcast(I32), -1.0, RSQRT_SEED, ALU.mult, ALU.add, w)
            for _ in range(NEWTON_STEPS):
                if q is pool:
                    w = tt(pool, s, r, r, ALU.mult, w)
                    w = tt(pool, s, s, ve, ALU.mult, w)
                    w = ts(pool, s, s, -0.5, 1.5, ALU.mult, ALU.add, w)
                    w = tt(pool, r, r, s, ALU.mult, w)
                else:
                    w = stt(dve, s, r, -0.5, r, ALU.mult, ALU.mult, w)
                    w = tt(dve, s, s, ve, ALU.mult, w)
                    w = stt(dve, r, s, 1.5, r, ALU.add, ALU.mult, w)
            return r, w, slot

        def statistics(src, tiles, *waits, eps=LN_EPS, q=None):
            n = len(tiles)
            bn = bn_ring.next()
            w = bn.free
            for i, t in enumerate(tiles):
                w = [dve.add(lambda e, i=i, t=t: e.bn_stats(bn.t[:, i, 0:6], src(t)), w, *waits)]
            last_stats = w
            for i, t in enumerate(tiles):
                w = [dve.add(lambda e, i=i: e.bn_aggr(bn.t[:, i, 6:8], bn.t[:, i, 0:6]), last_stats)]
            r, w_r, slot = rsqrt(bn.t[:, 0:n, 7], n, eps, w, q=q)
            return src, tiles, bn, r, slot, w_r

        def normalise(stats, dst):
            src, tiles, bn, r, slot, w_r = stats
            done = []
            for i, t in enumerate(tiles):
                done.append(ts(dve, dst(t), src(t), bn.t[:, i, 6:7], r[:, i:i + 1], ALU.subtract, ALU.mult, w_r))
            slot.free = bn.free = done[-1:]
            return done

        def down_projections():
            w_qn, w_key = [None] * NT, [None] * NT
            for h in range(NHALF):
                tiles = range(h * TH, (h + 1) * TH)
                w_copy, w_sq = [], None
                for t in tiles:
                    bank = banks[t]
                    w = mm(bank.t[:, 0:Q0 + QLR], [(xT[:, c, t * P:(t + 1) * P], w_down0[:, c, :]) for c in range(DC)],
                           l_xT, l_low, bank.free)
                    w = (act_op(low[:, t, 0:Q0 + QLR], bank.t[:, 0:Q0 + QLR], ACT.Copy, w) if t % 2 == 0 else
                         dve.add(lambda e, t=t, bank=bank: e.tensor_copy(low[:, t, 0:Q0 + QLR],
                                                                         bank.t[:, 0:Q0 + QLR]), w))
                    bank.free = [w]
                    w_copy.append(w)
                    for i, (lo_, hi_) in enumerate(((Q0, Q0 + QLR), (0, KVLR))):
                        part, total = low[:, t, lo_:hi_], sums[:, h, i, t - tiles[0]:t - tiles[0] + 1]
                        w_sq = dve.add(lambda e, part=part, i=i, total=total, n=hi_ - lo_: e.tensor_tensor_reduce(
                            out=square[:, i, 0:n], in0=part, in1=part, scale=1.0 / n, scalar=0.0,
                            op0=ALU.mult, op1=ALU.add, accum_out=total), w, w_sq)
                rot = low[:, tiles[0]:tiles[0] + TH, KVLR:Q0].rearrange("p (b t) d -> p b t d", t=TB)
                cos_part, sin_part = (rope_tmp[:, i, tiles[0]:tiles[0] + TH, :].rearrange("p (b t) d -> p b t d", t=TB)
                                      for i in range(2))

                def row(j, lo_, hi_):
                    return rope0[:, :, j, lo_:hi_].unsqueeze(1).to_broadcast([P, TH // TB, TB, hi_ - lo_])

                hd = DR // 2
                wa = tt(pool, cos_part, rot, row(0, 0, DR), ALU.mult, w_copy, l_const)
                tt(pool, sin_part[:, :, :, 0:hd], rot[:, :, :, hd:DR], row(1, 0, hd), ALU.mult)
                wb = tt(pool, sin_part[:, :, :, hd:DR], rot[:, :, :, 0:hd], row(1, hd, DR), ALU.mult)
                key_rot = key_tok[:, tiles[0]:tiles[0] + TH, KVLR:].rearrange("p (b t) d -> p b t d", t=TB)
                w_rot = tt(pool, key_rot, cos_part, sin_part, ALU.add, wa, wb)
                r, w_r, slot = rsqrt(sums[:, h, :, :].rearrange("p a t -> p (a t)"), 2 * TH, 1e-6, w_sq)
                if h == NHALF - 1:
                    yield
                for i, t in enumerate(tiles):
                    q, twice = low[:, t, Q0:Q0 + QLR], low[:, t, Q0 + QLR:]
                    w_twice = ts(pool, twice, q[:, P:], r[:, i:i + 1], 1.0, ALU.mult, ALU.mult, w_r, w_copy[i])
                    w_qn[t] = [act_op(q, q, ACT.Copy, w_r, w_copy[i], w_twice, scale=r[:, i:i + 1]), w_twice]
                    w_lat = stt(dve, key_tok[:, t, 0:KVLR], low[:, t, 0:KVLR], r[:, TH + i:TH + i + 1],
                                kv_ln[:, :], ALU.mult, ALU.mult, w_r, l_const, w_copy[i])
                    w_key[t] = [w_lat, w_rot]
                slot.free = w_qn[tiles[-1]] + [w_lat]
            w_qaT, w_keyT = [], []
            for h in range(NHALF):
                tiles = range(h * TH, (h + 1) * TH)
                for c in range(2):
                    bank = banks[2 * c + h]
                    for i, t in enumerate(tiles):
                        w = transpose(bank.t[:, i * P:(i + 1) * P], low[:, t, Q0 + c * P:Q0 + (c + 1) * P],
                                      w_qn[t], l_ident, bank.free, signal=True)
                    cols = slice(h * HALF, (h + 1) * HALF)
                    w_hi = act_op(qaT.hi[:, c, cols], bank.t[:, :], ACT.Copy, w, l_const, scale=q_ln[:, c:c + 1])
                    n = (P, QREST)[c]
                    w_lo = stt(dve, qaT.lo[0:n, c, cols], bank.t[0:n, :], q_ln[0:n, c:c + 1],
                               plain(qaT.hi[0:n, c, cols]), ALU.mult, ALU.subtract, w_hi)
                    bank.free = [w_lo]
                    w_qaT += [w_hi, w_lo]
                bank = banks[6 + h]
                for i, t in enumerate(tiles):
                    w = transpose(bank.t[:, i * P:(i + 1) * P], key_tok[:, t, :], w_key[t], bank.free, signal=True)
                w_keyT.append(act_op(keyT[:, h * HALF:(h + 1) * HALF], bank.t[:, :], ACT.Copy, w))
                bank.free = [w_keyT[-1]]
            ready["down"] = w_qaT, w_keyT, [w for k in w_key for w in k]
            yield

        group_weights = {}

        def prepare_group_weights(g):
            slot, w_q_in, w_v_in = raw0[g]
            nope, k_lat, rot, v_lat, o = raw_views(slot)
            dst = w_ring.next()
            n_q = 2 * GH * P
            w_q = Pair(*(t[:, 0:n_q].rearrange("p (c h d) -> p c h d", c=2, h=GH) for t in (dst.t.hi, dst.t.lo)))
            w_out = Pair(*(t[:, n_q:].rearrange("p (j n) -> p j n", n=D) for t in (dst.t.hi, dst.t.lo)))
            w_rot = split_query_weights(pool, w_q[:, :, :, KVLR:], rot, w_q_in, dst.free)
            bank = trans.next()
            out = bank.t[:, :].rearrange("p (c h d) -> p c h d", c=2, h=GH)
            for i in range(GH):
                mm(out[:, 0, i, :], [(nope[:, i, 0:P], k_lat[:, i, :])], w_q_in, bank.free, signal=False)
                for at in (0, QREST):
                    w = mm(out[at:at + QREST, 1, i, :], [(nope[:, i, P:], k_lat[:, i, :])], shared=True)
            w_abs = split_query_weights(dve, w_q[:, :, :, 0:KVLR], out, w, dst.free)
            bank.free = w_abs[-1:]
            yield
            bank = trans.next()
            for i in range(GH):
                half = i % 2
                w = mm(bank.t[half * KVLR:(half + 1) * KVLR, (i // 2) * D:(i // 2 + 1) * D],
                       [(v_lat[:, i, :], o[:, i, :])], w_v_in, bank.free, shared=True)
            w_vo = split_psum(w_out[:, :, :], bank.t[:, :].rearrange("p (j n) -> p j n", n=D), w, dst.free)
            bank.free = w_vo[-1:]
            slot.free = [w] + w_rot
            group_weights[g] = (dst, w_q, w_out, w_rot + w_abs, w_vo)
            if g + 2 < NG:
                load_group_weights(g + 2)
            else:
                load_expert(g + 2 - NG)
                if g + 2 == NG:
                    background.append(load_experts_front())
            yield

        down = down_projections()
        next(down)
        list(prepare_group_weights(0))
        next(down)
        w_qaT, w_keyT, w_key = ready["down"]
        front_read = w_qaT + w_keyT + w_key
        memory_front.close()
        scope[0] = (memory0, "left")
        q_tok_ring = ring("q_tok", 3, [P, GH, P])
        rope_ring = ring("rope_buf", 2, [P, 2, GH, DR])
        qT_ring = ring("qT", 3, [P, GH, S])
        for r in (q_tok_ring, rope_ring, qT_ring):
            for slot in r.slots:
                slot.free = list(front_read)
        SCALE0 = float(DQK) ** -0.5

        def exponentials(bank, w_scores, regions, scale):
            p, st = p_ring.next(), soft_ring.next()
            top, total = st.t[:, 0, :], st.t[:, 1, :]
            w_top, w_exp = [], []
            for i, (cols, mask) in enumerate(regions):
                w_top.append(dve.add(lambda e, i=i, cols=cols, mask=mask: e.tensor_tensor_reduce(
                    out=p.t[:, cols], in0=bank.t[:, cols], in1=mask, scale=-scale, scalar=3.0e38,
                    op0=ALU.add, op1=ALU.min, accum_out=top[:, i:i + 1]), w_scores, p.free, st.free))
            bank.free = w_top[-1:]
            for i, (cols, _) in enumerate(regions):
                w_exp.append(act_op(p.t[:, cols], p.t[:, cols], ACT.Exp, w_top[i], bias=top[:, i:i + 1], scale=-1.0,
                                    accum_out=total[:, i:i + 1]))
            return p, st, regions, w_exp

        def normalised(front, engines):
            p, st, regions, w_exp = front
            inv = st.t[:, 2, :]
            w_inv = dve.add(lambda e: e.reciprocal(inv, st.t[:, 1, :]), w_exp)
            done = [ts(q, p.t[:, cols], p.t[:, cols], inv[:, i:i + 1], 1.0, ALU.mult, ALU.mult, w_inv)
                    for i, ((cols, _), q) in enumerate(zip(regions, engines))]
            st.free = done
            return p, done

        y_token = {}

        def attention_group(b, g):
            tiles = [TB * b + i for i in range(TB)]
            w_slot, w_q, w_out, w_q_done, w_out_done = group_weights[g]
            qT = qT_ring.next()
            q_toks = []
            pbanks = [proj.next() for _ in tiles]
            for i, t in enumerate(tiles):
                bank = pbanks[i]
                cols = slice(t * P, (t + 1) * P)
                w = w_proj = mm(bank.t[:, :], [(qaT[:, 0, cols], w_q[:, 0, :, :]),
                                               (qaT.hi[:, 1, cols], w_q.hi[:, 1, :, :]),
                                               (qaT.lo[0:QREST, 1, cols], w_q.hi[0:QREST, 1, :, :])],
                                w_q_done, w_qaT, bank.free)
                q, rp = q_tok_ring.next(), rope_ring.next()
                view = bank.t[:, :].rearrange("p (h d) -> p h d", d=P)
                lat, rot = view[:, :, 0:KVLR], view[:, :, KVLR:]
                hd = DR // 2
                cos = rope0[:, i, 0, :].unsqueeze(1).to_broadcast([P, GH, DR])
                sin_lo = rope0[:, i, 1, 0:hd].unsqueeze(1).to_broadcast([P, GH, hd])
                sin_hi = rope0[:, i, 1, hd:DR].unsqueeze(1).to_broadcast([P, GH, hd])
                w1 = tt(dve, rp.t[:, 0, :, :], rot, cos, ALU.mult, w, rp.free)
                tt(dve, rp.t[:, 1, :, 0:hd], rot[:, :, hd:DR], sin_lo, ALU.mult)
                w2 = tt(dve, rp.t[:, 1, :, hd:DR], rot[:, :, 0:hd], sin_hi, ALU.mult)
                w_rot = tt(pool, q.t[:, :, KVLR:], rp.t[:, 0, :, :], rp.t[:, 1, :, :], ALU.add, w1, w2, q.free)
                rp.free = [w_rot]
                w_lat = act_op(q.t[:, :, 0:KVLR], lat, ACT.Copy, w, w2, q.free)
                bank.free = [w_lat]
                q_toks.append((q, w_lat, w_rot))
            if g == NG - 1:
                xT_free[b] = [w_proj]
            to_expert = g + 2 - NG if b == B - 1 and g + 2 >= NG else None
            if to_expert is not None:
                for i in range(2):
                    split_expert(to_expert, i, w_proj)
            yield
            w_qT = []
            for i, (q, w_lat, w_rot) in enumerate(q_toks):
                bank = pbanks[i]
                for h in range(GH):
                    w = transpose(bank.t[:, h * P:(h + 1) * P], q.t[:, h, :], w_lat, w_rot, bank.free,
                                  signal=h == GH - 1)
                q.free = [w]
                w_qT.append(act_op(qT.t[:, :, i * P:(i + 1) * P], bank.t[:, :].rearrange("p (h s) -> p h s", s=P),
                                   ACT.Copy, w, qT.free))
                bank.free = [w_qT[-1]]
            yield
            fronts, probs = [], []
            keys = keyT[:, b * S:(b + 1) * S]
            for h in range(GH):
                bank = score.next()
                mm(bank.t[:, 0:S], [(qT.t[:, h, P:S], keys)], w_qT, w_keyT, bank.free, signal=False)
                w = mm(bank.t[:, S:S + P], [(qT.t[:, h, 0:P], keys[:, 0:P])])
                fronts.append(exponentials(bank, w, [(slice(0, S), mask0[:, :]), (slice(S, S + P), mask0[:, P:S])],
                                           SCALE0))
                if h == 1:
                    yield
            qT.free = [w]
            probs += [normalised(f, (pool, pool)) for f in fronts[:2]]
            yield
            probs += [normalised(f, (pool, pool)) for f in fronts[2:]]
            pTs = []
            for h, (p, w_p) in enumerate(probs):
                bank, pT = trans.next(), pT_ring.next()
                transpose(bank.t[:, 0:P], p.t[:, S:S + P], w_p, bank.free)
                transpose(bank.t[:, P:2 * P], p.t[:, 0:P])
                w = transpose(bank.t[:, 2 * P:3 * P], p.t[:, P:S], signal=True)
                p.free = [w]
                w = act_op(pT.t[:, 0:3 * P], bank.t[:, 0:3 * P], ACT.Copy, w, pT.free)
                bank.free = [w]
                pTs.append((pT, w))
                if h == 1:
                    yield
            yield
            bank = pv_bank
            for h, (pT, w_pT) in enumerate(pTs):
                out = bank.t[(h % 2) * KVLR:(h % 2 + 1) * KVLR, (h // 2) * S:(h // 2 + 1) * S]
                mm(out, [(key_tok[:, tiles[0], 0:KVLR], pT.t[:, 0:S])], w_pT, w_key, bank.free,
                   stop=False, shared=True, signal=False)
                w = mm(out[:, P:S], [(key_tok[:, tiles[1], 0:KVLR], pT.t[:, S:S + P])], start=False, shared=True)
                pT.free = [w]
            ctxp = ctx_pair_ring.next()
            w_ctx = split_psum(Pair(ctxp.t.hi[:, :, :], ctxp.t.lo[:, :, :]),
                               bank.t[:, :].rearrange("p (a s) -> p a s", s=S), w, ctxp.free)
            bank.free = w_ctx[-1:]
            yield
            for i in range(TB):
                terms = [(ctxp.t[:, j, i * P:(i + 1) * P], w_out[:, j, :]) for j in range(2)]
                w = mm(acc_bank.t[:, i * D:(i + 1) * D], terms, w_ctx, w_out_done, acc_bank.free)
            ctxp.free = [w]
            if b == B - 1:
                w_slot.free = [w]
            if to_expert is not None:
                split_expert(to_expert, 2, w)
            rows = slice(TB * b, TB * b + TB)
            before = x if g == 0 else y
            y_token[b] = tt(dve, y[:, rows, :], acc_bank.t[:, :].rearrange("p (t d) -> p t d", d=D),
                            before[:, rows, :], ALU.add, w, l_x, y_token.get(b))
            acc_bank.free = [y_token[b]]
            if g == NG - 1:
                background.append(finish_attention0(b, y_token[b]))
            yield

        gate_tokens = []

        def learned_adjacency():
            w = act_op(gate_col[:, 1:2], gate_col[:, 0:1], ACT.Exp, l_x0, scale=-1.0)
            w = ts(dve, gate_col[:, 1:2], gate_col[:, 1:2], 1.0, None, ALU.add, None, w)
            w = dve.add(lambda e: e.reciprocal(gate_col[:, 1:2], gate_col[:, 1:2]), w)
            w1 = ts(dve, gate_col[:, 2:3], gate_col[:, 1:2], 0.5, None, ALU.mult, None, w)
            w2 = ts(dve, gate_col[:, 3:4], gate_col[:, 1:2], -1.0, 1.0, ALU.mult, ALU.add, w)
            gate_tokens.extend([w1, w2])
            w_qk = []
            for i in range(2):
                for h in range(NHALF):
                    bank = trans.next()
                    cols = slice(h * HALF, (h + 1) * HALF)
                    w = mm(bank.t[0:CTX, :], [(w_qk_x[:, i, :], ctxT[:, cols])], l_x0, l_ctx, bank.free)
                    w_qk.append(act_op(qk_x[:, i, cols], bank.t[0:CTX, :], ACT.Copy, w))
                    bank.free = w_qk[-1:]
                yield
            for b in range(B):
                w_adj, rows = [], []
                for i in range(TB):
                    t = TB * b + i
                    s, best, bank = sim_ring.next(), best_ring.next(), trans.next()
                    w = mm(bank.t[:, 0:S], [(qk_x[:, 0, t * P:(t + 1) * P], qk_x[:, 1, b * S:(b + 1) * S])],
                           w_qk, bank.free)
                    sim, work, sig = s.t[:, 0, :], s.t[:, 1, :], s.t[:, 2, :]
                    w_sim = act_op(sim, bank.t[:, 0:S], ACT.Copy, w, s.free)
                    bank.free = [w_sim]
                    w_sig = act_op(sig, sim, ACT.Exp, w_sim, s.free, scale=-1.0 / 16)
                    rows.append([s, best, sim, work, sig, w_sim, w_sig])
                yield
                for k in range((TOPK - 1) // 8 + 1):
                    for row in rows:
                        s, best, sim, work, _, w, _ = row
                        src = work if k else sim
                        row[5] = dve.add(lambda e, src=src, best=best: e.max(best.t[:, :], src), w, best.free, s.free)
                    if k < (TOPK - 1) // 8:
                        for row in rows:
                            s, best, sim, work, _, w, _ = row
                            src = work if k else sim
                            row[5] = dve.add(lambda e, src=src, work=work, best=best: e.match_replace(
                                out=work, in_to_replace=best.t[:, :], in_values=src, imm_value=-3.0e38), w)
                    yield
                for i, (s, best, sim, work, sig, w, w_sig) in enumerate(rows):
                    w_sig = ts(dve, sig, sig, 1.0, None, ALU.add, None, w_sig)
                    w_sig = dve.add(lambda e, sig=sig: e.reciprocal(sig, sig), w_sig)
                    at = (TOPK - 1) % 8
                    w = stt(dve, adjacency[:, TB * b + i, :], sim, best.t[:, at:at + 1], sig, ALU.is_ge, ALU.mult,
                            w, w_sig)
                    s.free = best.free = [w]
                    w_adj.append(w)
                    yield
                bank = trans.next()
                for i in range(TB):
                    for j in range(TB):
                        w = transpose(bank.t[:, i * S + j * P:i * S + (j + 1) * P],
                                      adjacency[:, TB * b + j, i * P:(i + 1) * P], w_adj, bank.free, signal=True)
                rows = slice(TB * b, TB * b + TB)
                w = tt(dve, adjacency[:, rows, :], bank.t[:, :].rearrange("p (t d) -> p t d", d=S),
                       adjacency[:, rows, :], ALU.add, w)
                bank.free = [w]
                ready["adjacency", b] = w
                yield
            ready["adjacency_done"] = True

        def context_keys():
            bank = trans.next()
            view = bank.t[:, :].rearrange("p (t d) -> p t d", d=CTX)
            for t in range(NT):
                w = mm(view[:, t, :], [(ctxT[:, t * P:(t + 1) * P], w_kv_x[:, :])], l_x0, l_ctx, bank.free,
                       signal=t == NT - 1)
            w1 = tt(dve, kv_tok[:, :, :], view, kv_bias_row[:, :].unsqueeze(1).to_broadcast([P, NT, CTX]), ALU.add, w)
            bank.free = [w1]
            tokens = [w1]
            yield
            for h in range(NHALF):
                bank = trans.next()
                cols = slice(h * HALF, (h + 1) * HALF)
                w = mm(bank.t[0:CTX, :], [(w_kv_x[:, :], ctxT[:, cols])], bank.free)
                tokens.append(act_op(kvT[:, cols], bank.t[0:CTX, :], ACT.Identity, w, bias=kv_bias_col[:, 0:1]))
                bank.free = tokens[-1:]
            ready["context_keys"] = tokens
            yield

        xT_free = [[] for _ in range(B)]

        def transpose_x(b, w_x, dst=None):
            bank = trans.next()
            for c in range(DC):
                for i in range(TB):
                    w = transpose(bank.t[:, c * S + i * P:c * S + (i + 1) * P],
                                  x[:, TB * b + i, c * P:(c + 1) * P], w_x, bank.free, signal=True)
            cols = slice(b * S, (b + 1) * S)
            view = bank.t[:, :].rearrange("p (c s) -> p c s", s=S)
            if dst is not None:
                tokens = [act_op(dst[:, :, cols], view, ACT.Copy, w, xT_free[b])]
            else:
                tokens = split_psum(Pair(xT_pair.hi[:, :, cols], xT_pair.lo[:, :, cols]), view, w, xT_free[b])
            bank.free = tokens[-1:]
            return tokens

        def x_tile(t):
            return x[:, t, :]

        def y_tile(t):
            return y[:, t, :]

        def finish_attention0(b, w_y):
            tiles = [TB * b + i for i in range(TB)]
            stats = statistics(y_tile, tiles, w_y, q=pool)
            yield
            w_x = normalise(stats, x_tile)
            w_adj = given(("adjacency", b))
            w_mix = []
            for t in tiles:
                w = stt(dve, y[:, t, :], x[:, t, :], gate_col[:, 3:4], x[:, t, :], ALU.mult, ALU.add,
                        w_x, gate_tokens)
                w_mix.append(stt(dve, y[:, t, :], adjacency[:, t, :], gate_col[:, 2:3], y[:, t, :],
                                 ALU.mult, ALU.add, w, w_adj))
            stats = statistics(y_tile, tiles, w_mix, q=pool)
            yield
            w_x = normalise(stats, x_tile)
            yield
            ready["xT_experts", b] = transpose_x(b, w_x)
            ready["x_experts", b] = w_x
            yield
            yield from router(b)

        w_e_loaded, w_e = {}, {}

        def expert_views(t):
            return t[:, 0:3 * DC * D].rearrange("p (i c n) -> p i c n", i=3, c=DC)

        def load_expert(e):
            slot = raw_ring.next()
            view = expert_views(slot.t)
            names = (("L0_ffn_Wsu", "L0_ffn_Wsg", "L0_ffn_Wsd") if e == E_ROUTED else
                     ("L0_ffn_Wup", "L0_ffn_Wgate", "L0_ffn_Wdown"))
            srcs = [a[n] if e == E_ROUTED else a[n][e, :, :] for n in names]
            w_e_loaded[e] = (slot, load([(view[:, i, :, :], s.rearrange("(c p) n -> p c n", p=P))
                                         for i, s in enumerate(srcs)], slot.free))

        def split_expert(e, i, free):
            raw, w_load = w_e_loaded[e]
            if i == 0:
                slot = w_e[e - 2][0] if e >= 2 else group_weights[NG - 2 + e][0]
                w_e[e] = (slot, Pair(expert_views(slot.t.hi), expert_views(slot.t.lo)), {})
            slot, views, tokens = w_e[e]
            tokens[i] = split_sbuf(views[:, i, :, :], expert_views(raw.t)[:, i, :, :], w_load, free)
            if i == 2:
                raw.free = tokens[i]
                if e + 2 < NE:
                    load_expert(e + 2)
                elif e + 2 == NE:
                    load_qkv()
                else:
                    load_ffn(0)

        def matrix_read(e, i, h, w):
            if h == NHALF - 1 and e + 2 < NE:
                split_expert(e + 2, i, w)

        def load_experts_front():
            z = pool.add(lambda e: e.memset(w_router_in[:, :, :], 0.0))
            z2 = pool.add(lambda e: e.memset(router_rows[:, :, :], 0.0))
            wl = load([(w_router_in[:, :, 0:E_ROUTED], a["L0_ffn_Wr"].rearrange("(c p) n -> p c n", p=P)),
                       (router_rows[:, 0, 0:E_ROUTED], a["L0_ffn_br"].partition_broadcast(P)),
                       (router_rows[:, 1, 0:E_ROUTED], a["L0_ffn_gate_bias"].partition_broadcast(P)),
                       (iota[:, :], a["iota"]),
                       (b_down[0:E_ROUTED, :], a["L0_ffn_bdown"]), (b_down[E_ROUTED:NE, :], a["bsd_row"]),
                       (b_up[:, 0:E_ROUTED, :], a["bup_cols"]), (b_up[:, E_ROUTED, :], a["bsu_cols"]),
                       (b_gate[:, 0:E_ROUTED, :], a["bgate_cols"]), (b_gate[:, E_ROUTED, :], a["bsg_cols"])],
                      z, z2)
            ready["router"] = (wl, split_sbuf(Pair(w_router.hi[:, :, :], w_router.lo[:, :, :]),
                                              w_router_in[:, :, :], wl))
            yield

        def router(b):
            tiles = [TB * b + i for i in range(TB)]
            wl, w_w = given("router")
            w_xT = given(("xT_experts", b))
            rt = router_ring.next()
            gate, bias, pick, tmp = (rt.t[:, i, :, :] for i in range(4))
            idx, stat = rt_idx.next(), rt_stat.next()
            bank = trans.next()
            view = bank.t[:, 0:TB * NE].rearrange("p (t e) -> p t e", e=NE)
            for i, t in enumerate(tiles):
                w = mm(view[:, i, :], [(xT_pair[:, c, t * P:(t + 1) * P], w_router[:, c, :]) for c in range(DC)],
                       w_xT, w_w, bank.free, signal=i == TB - 1)
            rows = [router_rows[:, j, :].unsqueeze(1).to_broadcast([P, TB, NE]) for j in range(2)]
            w = tt(dve, gate, view, rows[0], ALU.add, w, wl, rt.free)
            bank.free = [w]
            w_gate = w
            w = tt(dve, bias, gate, rows[1], ALU.add, w)
            w = dve.add(lambda e: e.memset(bias[:, :, E_ROUTED:], -3.0e38), w)
            for i in range(TB):
                w8 = dve.add(lambda e, i=i: e.max(stat.t[:, i, :], bias[:, i, :]), w, stat.free)
                w_i = dve.add(lambda e, i=i: e.max_index(idx.t[:, i, :], stat.t[:, i, :], bias[:, i, :]), w8, idx.free)
            w = dve.add(lambda e: e.tensor_copy(stat.t[:, :, 0:2], idx.t[:, :, 0:2]), w_i)
            for i in range(TB):
                w1 = ts(dve, pick[:, i, :], iota[:, :], stat.t[:, i, 0:1], None, ALU.is_equal, None, w, wl)
                w2 = stt(dve, pick[:, i, :], iota[:, :], stat.t[:, i, 1:2], pick[:, i, :], ALU.is_equal, ALU.add, w1)
            yield
            w = ts(dve, tmp, pick, -NEG, NEG, ALU.mult, ALU.add, w2)
            w_m = tt(dve, tmp, tmp, gate, ALU.add, w, w_gate)
            w = dve.add(lambda e: e.reduce_max(stat.t[:, :, 2], tmp, mybir.AxisListType.X), w_m)
            w = tt(dve, tmp, tmp, stat.t[:, :, 2:3].to_broadcast([P, TB, NE]), ALU.subtract, w)
            w = act_op(tmp, tmp, ACT.Exp, w)
            w = dve.add(lambda e: e.reduce_sum(stat.t[:, :, 3], tmp, mybir.AxisListType.X), w)
            w = dve.add(lambda e: e.reciprocal(stat.t[:, :, 3], stat.t[:, :, 3]), w)
            rows_b = slice(TB * b, TB * b + TB)
            w = tt(dve, probs_e[:, rows_b, :], tmp, stat.t[:, :, 3:4].to_broadcast([P, TB, NE]), ALU.mult, w)
            w_p = dve.add(lambda e: e.memset(probs_e[:, rows_b, E_ROUTED:], 1.0), w)
            rt.free = idx.free = stat.free = [w_p]
            yield
            bank = trans.next()
            for i, t in enumerate(tiles):
                w = transpose(bank.t[0:NE, i * P:(i + 1) * P], probs_e[:, t, :], w_p, bank.free, signal=True)
            pe_T = probs_eT_ring.next()
            w_pT = dve.add(lambda e, bank=bank: e.tensor_copy(pe_T.t[:, :], bank.t[0:NE, 0:S]), w, pe_T.free)
            bank.free = [w_pT]
            yield
            bank = trans.next()
            for i, t in enumerate(tiles):
                w = mm(bank.t[:, i * D:(i + 1) * D], [(pe_T.t[:, i * P:(i + 1) * P], b_down[:, :])],
                       w_pT, wl, bank.free)
            w = tt(dve, y[:, rows_b, :], bank.t[:, :].rearrange("p (t d) -> p t d", d=D), x[:, rows_b, :],
                   ALU.add, w, given(("x_experts", b)))
            bank.free = pe_T.free = [w]
            ready["router", b] = [w, w_p]
            yield

        acc_tokens = {}

        def expert(e, h):
            w_x = [w for b in range(TB * h, TB * h + 2) for w in need(("xT_experts", b))]
            w_slot, wp, w_w = w_e[e]
            cols = slice(h * HALF, (h + 1) * HALF)
            u, up = [p_ring.next() for _ in range(DC)], u_pair.next()
            w_u, w_up = [], []
            for i in range(DC):
                bank = banks[i]
                w = mm(bank.t[:, :], [(wp[:, 0, c, i * P:(i + 1) * P], xT_pair[:, c, cols]) for c in range(DC)],
                       w_w[0], w_x, bank.free)
                bias = b_up[:, e, i:i + 1]
                w_hi = act_op(up.t.hi[:, i, :], bank.t[:, :], ACT.Identity, w, up.free, bias=bias)
                w_u.append(act_op(u[i].t[:, :], bank.t[:, :], ACT.Identity, w, u[i].free, bias=bias))
                w_lo = tt(dve, up.t.lo[:, i, :], u[i].t[:, :], plain(up.t.hi[:, i, :]), ALU.subtract, w_u[i], up.free)
                bank.free = [w_u[i]]
                w_up += [w_hi, w_lo]
            matrix_read(e, 0, h, w)
            if e == NE - 1:
                for b in (2 * h, 2 * h + 1):
                    xT_free[b] = [w]
            yield
            sl, gp = [p_ring.next() for _ in range(DC)], g_pair.next()
            w_m = []
            for j in range(DC):
                bank = banks[2 + j]
                w = mm(bank.t[:, :], [(wp[:, 1, c, j * P:(j + 1) * P], up.t[:, c, :]) for c in range(DC)],
                       w_w[1], w_up, bank.free)
                w_s = act_op(sl[j].t[:, :], bank.t[:, :], ACT.Silu, w, sl[j].free, bias=b_gate[:, e, j:j + 1])
                bank.free = [w_s]
                w_m.append(tt(pool, sl[j].t[:, :], sl[j].t[:, :], u[j].t[:, :], ALU.mult, w_s, w_u))
                u[j].free = [w_up[2 * j + 1], w_m[j]]
            matrix_read(e, 1, h, w)
            up.free = [w]
            yield
            w_g = []
            for j in range(DC):
                w_hi = act_op(gp.t.hi[:, j, :], sl[j].t[:, :], ACT.Copy, w_m[j], gp.free)
                w_lo = tt(dve, gp.t.lo[:, j, :], sl[j].t[:, :], plain(gp.t.hi[:, j, :]), ALU.subtract, w_hi, gp.free)
                w_g += [w_hi, w_lo]
                sl[j].free = [w_lo]
            yield
            for i in range(TH // 2):
                bank = banks[6 + i]
                for j in range(2):
                    t = h * TH + 2 * i + j
                    w = mm(bank.t[:, j * D:(j + 1) * D],
                           [(gp.t[:, c, (2 * i + j) * P:(2 * i + j + 1) * P], wp[:, 2, c, :]) for c in range(DC)],
                           w_w[2], w_g, bank.free)
                for j in range(2):
                    t = h * TH + 2 * i + j
                    w_r = need(("router", t // TB))
                    w_acc = stt(dve, y[:, t, :], bank.t[:, j * D:(j + 1) * D], probs_e[:, t, e:e + 1],
                                y[:, t, :], ALU.mult, ALU.add, w, w_r, acc_tokens.get(t))
                    acc_tokens[t] = w_acc
                bank.free = [w_acc]
            gp.free = [w]
            matrix_read(e, 2, h, w)
            if h == NHALF - 1 and e + 2 >= NE:
                w_slot.free = [w]
                if e + 2 == NE:
                    split_qkv()
                else:
                    for part in range(2):
                        split_ffn(0, part, None)
            if e == NE - 1:
                background.append(finish_experts(h))
            yield

        def finish_experts(h):
            tiles = range(h * TH, (h + 1) * TH)
            stats = statistics(y_tile, tiles, [acc_tokens[t] for t in tiles], q=pool)
            yield
            w_x = normalise(stats, x_tile)
            yield
            for _ in range(2 * h):
                yield
            for i in range(2):
                b = 2 * h + i
                ready["xT_attn1", b] = transpose_x(b, w_x[TB * i:TB * (i + 1)])
                ready["x_attn1", b] = w_x[TB * i:TB * (i + 1)]
                yield

        SCALE1 = float(HD1) ** -0.5

        def load_qkv():
            slot = raw_ring.next()
            raw = slot.t[:, 0:3 * DC * D].rearrange("p (c n) -> p c n", c=DC)
            ready["qkv_in"] = (slot, raw, load([(raw, a["L1_attn_Wqkv"].rearrange("(c p) n -> p c n", p=P))],
                                               slot.free))

        def split_qkv():
            slot, raw, wl = ready["qkv_in"]
            dst = w_ring.next()
            w_qkv = Pair(*(t[:, :].rearrange("p (c n) -> p c n", c=DC) for t in (dst.t.hi, dst.t.lo)))
            got = split_sbuf(w_qkv[:, :, :], raw, wl, dst.free)
            slot.free = got
            ready["w_qkv"] = (dst, w_qkv, got)
            load_ffn(1)

        def load_attn1():
            z = pool.add(lambda e: e.memset(w_out1[:, :, :], 0.0))
            src = a["L1_attn_Wout"].rearrange("(g j r) n -> j r g n", j=GH, r=HD1)
            return load([(b_qkv[:, :], a["L1_attn_bqkv"].partition_broadcast(P)),
                         (b_out1[:, :], a["L1_attn_bout"].partition_broadcast(P)),
                         (mask1[:, :, :], a["mask1"]), (rope1[:, :, :, :], a["rope1"]),
                         (row_mask[:, :], a["row_mask"]),
                         (ln_rows[:, 0, :], a["L1_xattn_ln_gamma"].partition_broadcast(P)),
                         (ln_rows[:, 1, :], a["L1_xattn_ln_beta"].partition_broadcast(P))]
                        + [(w_out1[j * HS1:j * HS1 + HD1, :, :], src[j]) for j in range(GH)], z)

        qkv_ready = {}

        def project_qkv(b):
            w_slot, w_qkv, w_w = ready["w_qkv"]
            w_xT = need(("xT_attn1", b))
            qT, kT, v_tok = q1_ring.next(), k1_ring.next(), v_ring.next()
            tiles = [TB * b + i for i in range(TB)]
            v_bank = trans.next()
            toks, cos_part, sin_part = [], pT_ring.next(), pT_ring.next()
            for i, t in enumerate(tiles):
                bank = front.next()
                xt = [xT_pair[:, c, t * P:(t + 1) * P] for c in range(DC)]
                w = mm(bank.t[:, :], [(xt[c], w_qkv[:, c, 0:2 * D]) for c in range(DC)], w_w, w_xT, bank.free)
                slot = p_ring.next()
                qk, r0, r1 = (s_.t[:, :].rearrange("p (h d) -> p h d", d=HD1) for s_ in (slot, cos_part, sin_part))
                w_b = tt(dve, qk, bank.t[:, :].rearrange("p (h d) -> p h d", d=HD1),
                         b_qkv[:, 0:2 * D].rearrange("p (h d) -> p h d", d=HD1), ALU.add, w, slot.free, w_attn1_const)
                bank.free = [w_b]
                hd = HD1 // 2

                def row(j, lo_, hi_):
                    return rope1[:, i, j, lo_:hi_].unsqueeze(1).to_broadcast([P, 2 * H1, hi_ - lo_])

                tt(dve, r1[:, :, 0:hd], qk[:, :, hd:HD1], row(1, 0, hd), ALU.mult, w_b, sin_part.free)
                w2 = tt(dve, r1[:, :, hd:HD1], qk[:, :, 0:hd], row(1, hd, HD1), ALU.mult)
                w1 = tt(pool, r0, qk, row(0, 0, HD1), ALU.mult, w_b, cos_part.free)
                w_q = tt(pool, qk, r0, r1, ALU.add, w1, w2)
                cos_part.free = sin_part.free = [w_q]
                toks.append((slot, w_q))
                wv_ = mm(v_bank.t[:, i * D:(i + 1) * D], [(xt[c], w_qkv[:, c, 2 * D:]) for c in range(DC)],
                         v_bank.free)
            xT_free[b] = [wv_]
            for i, t in enumerate(tiles):
                w_v = tt(dve, v_tok.t[:, i, :, 0:HD1],
                         v_bank.t[:, i * D:(i + 1) * D].rearrange("p (h d) -> p h d", d=HD1),
                         b_qkv[:, 2 * D:].rearrange("p (h d) -> p h d", d=HD1), ALU.add, wv_, v_tok.free, zeroed)
            v_bank.free = [w_v]
            yield
            got = []
            for i, (slot, w_q) in enumerate(toks):
                bank = front.next()
                for j in range(4):
                    w = transpose(bank.t[:, j * P:(j + 1) * P], slot.t[:, j * P:(j + 1) * P], w_q, bank.free,
                                  signal=j == 3)
                slot.free = [w]
                for n, dst in enumerate((qT, kT)):
                    got.append(act_op(dst.t[:, :, i * P:(i + 1) * P],
                                      bank.t[:, 2 * n * P:2 * (n + 1) * P].rearrange("p (g s) -> p g s", s=P),
                                      ACT.Copy, w, dst.free))
                bank.free = got[-1:]
            if b == B - 1:
                w_slot.free = [wv_]
                for part in range(2):
                    split_ffn(1, part, wv_)
            qkv_ready[b] = (qT, kT, v_tok, got + [w_v])
            yield

        def attention1_group(b, g):
            qT, kT, v_tok, w_qkv_done = qkv_ready[b]
            qm, tile = q1m_ring.next(), g * GH // HEADS_PER_TILE
            first = g * GH % HEADS_PER_TILE
            w_qm = tt(pool, qm.t[:, :, :], qT.t[:, tile, :].unsqueeze(1).to_broadcast([P, GH, S]),
                      row_mask[:, first:first + GH].unsqueeze(2).to_broadcast([P, GH, S]), ALU.mult,
                      w_qkv_done, w_attn1_const, qm.free)
            yield
            yield
            fronts, probs = [], []
            for h in range(GH):
                bank = front.next()
                for i in range(TB):
                    w = mm(bank.t[:, i * S:(i + 1) * S], [(qm.t[:, h, i * P:(i + 1) * P], kT.t[:, tile, :])],
                           w_qm, w_qkv_done, bank.free)
                fronts.append(exponentials(bank, w, [(slice(i * S, (i + 1) * S), mask1[:, i, :]) for i in range(TB)],
                                           SCALE1))
                if h == 1:
                    yield
            qm.free = [w]
            if g == G1 - 1:
                qT.free, kT.free = [w_qm], [w]
            probs += [normalised(f, (dve, pool)) for f in fronts[:2]]
            yield
            probs += [normalised(f, (dve, pool)) for f in fronts[2:]]
            pTs = []
            for h, (p, w_p) in enumerate(probs):
                bank, pT = trans.next(), pT_ring.next()
                for j in range(TB):
                    for i in range(TB):
                        w = transpose(bank.t[:, j * S + i * P:j * S + (i + 1) * P],
                                      p.t[:, i * S + j * P:i * S + (j + 1) * P], w_p, bank.free,
                                      signal=i == j == TB - 1)
                p.free = [w]
                w = act_op(pT.t[:, :], bank.t[:, :], ACT.Copy, w, pT.free)
                bank.free = [w]
                pTs.append((pT, w))
                if h == 1:
                    yield
            yield
            bank = pv_bank
            for h, (pT, w_pT) in enumerate(pTs):
                w = mm(bank.t[h * HS1:(h + 1) * HS1, 0:S],
                       [(v_tok.t[:, j, g * GH + h, :], pT.t[:, j * S:(j + 1) * S]) for j in range(TB)],
                       w_pT, bank.free, shared=True)
                pT.free = [w]
            if g == G1 - 1:
                v_tok.free = [w]
            c1 = ctx1_ring.next()
            w_c = act_op(c1.t[:, :], bank.t[:, 0:S], ACT.Copy, w, c1.free)
            bank.free = [w_c]
            yield
            for i in range(TB):
                w = mm(acc_bank.t[:, i * D:(i + 1) * D], [(c1.t[:, i * P:(i + 1) * P], w_out1[:, g, :])],
                       w_c, acc_bank.free if g == 0 else None, start=g == 0 and i == 0, stop=g == G1 - 1, shared=True)
            c1.free = [w]
            if g == G1 - 1:
                rows = slice(TB * b, TB * b + TB)
                w1 = tt(dve, y[:, rows, :], acc_bank.t[:, :].rearrange("p (t d) -> p t d", d=D), x[:, rows, :],
                        ALU.add, w, given(("x_attn1", b)))
                acc_bank.free = [w1]
                w1 = tt(dve, y[:, rows, :], y[:, rows, :], b_out1[:, :].unsqueeze(1).to_broadcast([P, TB, D]),
                        ALU.add, w1)
                background.append(bilinear(b, w1))
            yield

        def bilinear(b, w_y):
            tiles = [TB * b + i for i in range(TB)]
            stats = statistics(y_tile, tiles, w_y, q=pool)
            yield
            w_x = normalise(stats, x_tile)
            yield
            w_xT = transpose_x(b, w_x, dst=xT)
            if b < B - 1:
                yield
            w_k = given("context_keys")
            o, s, st = outT_ring.next(), bi_ring.next(), bi_stat.next()
            bank = trans.next()
            w = mm(bank.t[0:CTX, 0:S], [(kv_tok[:, tiles[c], :], xT[:, c, b * S:(b + 1) * S]) for c in range(DC)],
                   w_xT, w_k, bank.free)
            w_o = act_op(o.t[:, :], bank.t[0:CTX, 0:S], ACT.Copy, w, o.free)
            bank.free = [w_o]
            if b < B - 1:
                yield
            bank = trans.next()
            for i in range(TB):
                w = mm(bank.t[:, i * S:(i + 1) * S], [(o.t[:, i * P:(i + 1) * P], kvT[:, b * S:(b + 1) * S])],
                       w_o, w_k, bank.free)
            o.free = [w]
            w = act_op(s.t[:, :, :], bank.t[:, :].rearrange("p (t d) -> p t d", d=S), ACT.Copy, w, s.free,
                       scale=float(D) ** -0.5)
            bank.free = [w]
            yield

            def s_tile(t):
                return s.t[:, t - tiles[0], :]

            stats = statistics(s_tile, tiles, w, eps=1e-6, q=pool)
            yield
            w_n = normalise(stats, s_tile)
            rows = [ln_rows[:, j, :].unsqueeze(1).to_broadcast([P, TB, S]) for j in range(2)]
            w = tt(pool, s.t[:, :, :], s.t[:, :, :], rows[0], ALU.mult, w_n, w_attn1_const)
            w = tt(pool, s.t[:, :, :], s.t[:, :, :], rows[1], ALU.add, w)
            yield
            w = dve.add(lambda e: e.reduce_max(st.t[:, 0, :], s.t[:, :, :], mybir.AxisListType.X), w, st.free)
            w = ts(dve, st.t[:, 0, :], st.t[:, 0, :], -1.0, None, ALU.mult, None, w)
            yield
            for i in range(TB):
                w_e = act_op(s.t[:, i, :], s.t[:, i, :], ACT.Exp, w, bias=st.t[:, 0, i:i + 1],
                             accum_out=st.t[:, 1, i:i + 1])
            yield
            w = dve.add(lambda e: e.reciprocal(st.t[:, 2, :], st.t[:, 1, :]), w_e)
            w_m = []
            for i, t in enumerate(tiles):
                w_m.append(stt(dve, y[:, t, :], s.t[:, i, :], st.t[:, 2, i:i + 1], x[:, t, :], ALU.mult, ALU.add, w))
            s.free = st.free = w_m[-1:]
            stats = statistics(y_tile, tiles, w_m, q=pool)
            yield
            w_x = normalise(stats, x_tile)
            yield
            ready["xT_ffn", b] = transpose_x(b, w_x)
            ready["x_ffn", b] = w_x
            yield

        ffn_raw, ffn_w = {}, {}
        MT = 2

        def ffn_views(t):
            n = 2 * DC * MT * P
            return (t[:, 0:n].rearrange("p (i c n) -> p i c n", i=2, c=DC),
                    t[:, n:n + MT * D].rearrange("p (m n) -> p m n", n=D))

        def load_ffn(u):
            slot = raw_ring.next()
            gu, dn = ffn_views(slot.t)
            m = u % (HT // MT) * MT
            cols = slice(m * P, (m + MT) * P)
            ffn_raw[u] = (slot, load([(gu[:, i, :, :], a[name].rearrange("(c p) n -> p c n", p=P)[:, :, cols])
                                      for i, name in enumerate(("w_gateT", "w_upT"))]
                                     + [(dn, a["w_downT"].rearrange("(m p) n -> p m n", p=P)[:, m:m + MT, :])],
                                     slot.free))

        NU = NHALF * HT // MT

        def split_ffn(u, part, free):
            raw, wl = ffn_raw[u]
            if part == 0:
                slot = ffn_w[u - 2][0] if u >= 2 else w_ring.next()
                free = [free, slot.free]
                ffn_w[u] = (slot, {})
            slot, got = ffn_w[u]
            views = [Pair(hi, lo) for hi, lo in zip(ffn_views(slot.t.hi), ffn_views(slot.t.lo))]
            src = ffn_views(raw.t)
            if part == 0:
                got[0] = views[0], [split_sbuf(views[0][:, i, :, :], src[0][:, i, :, :], wl, free) for i in range(2)]
            else:
                got[1] = views[1], split_sbuf(views[1][:, :, :], src[1], wl, free)
                raw.free = got[1][1]
                if u + 2 < NU:
                    load_ffn(u + 2)

        def ffn(h, m):
            u = h * (HT // MT) + m // MT
            (w_gu, w_gu_done), (w_dn, w_dn_done) = (ffn_w[u][1][part] for part in range(2))
            w_x = [w for b in range(2 * h, 2 * h + 2) for w in need(("xT_ffn", b))]
            cols = slice(h * HALF, (h + 1) * HALF)
            rows = slice(m % MT * P, (m % MT + 1) * P)
            got = []
            for i in range(2):
                bank = banks[2 * (m % 2) + i]
                got.append((bank, mm(bank.t[:, :], [(w_gu[:, i, c, rows], xT_pair[:, c, cols]) for c in range(DC)],
                                     w_gu_done, w_x, bank.free)))
            (gate, w_gate), (up, w_up) = got
            sl = p_ring.next()
            w_s = act_op(sl.t[:, :], gate.t[:, :], ACT.Silu, w_gate, sl.free)
            gate.free = [w_s]
            w_m = tt(dve, sl.t[:, :], up.t[:, :], sl.t[:, :], ALU.mult, w_s, w_up)
            up.free = [w_m]
            last_of_pair = m % MT == MT - 1 and u + 2 < NU
            if last_of_pair:
                split_ffn(u + 2, 0, w_up)
            yield
            gp = g1_pair.next()
            w_hi = act_op(gp.t.hi[:, :], sl.t[:, :], ACT.Copy, w_m, gp.free)
            w_lo = tt(dve, gp.t.lo[:, :], sl.t[:, :], plain(gp.t.hi[:, :]), ALU.subtract, w_hi, gp.free)
            sl.free = [w_lo, w_hi]
            yield
            for i in range(TH):
                bank = banks[6 + i // 2]
                w = mm(bank.t[:, (i % 2) * D:(i % 2 + 1) * D],
                       [(gp.t[:, i * P:(i + 1) * P], w_dn[:, m % MT, :])], w_dn_done, w_hi, w_lo,
                       bank.free if m == 0 else None, start=m == 0 and i % 2 == 0, stop=m == HT - 1, shared=True)
            gp.free = [w]
            if last_of_pair:
                split_ffn(u + 2, 1, w)
            if m == HT - 1:
                for i in range(2):
                    bank, b = banks[6 + i], 2 * h + i
                    rows_b = slice(TB * b, TB * b + TB)
                    w_y = tt(dve, y[:, rows_b, :], bank.t[:, :].rearrange("p (t d) -> p t d", d=D), x[:, rows_b, :],
                             ALU.add, w, ready["x_ffn", b])
                    bank.free = [w_y]
                background.append(finish_ffn(h, w_y))
            yield

        def finish_ffn(h, w_y):
            stats = statistics(y_tile, range(h * TH, (h + 1) * TH), w_y, q=pool if h == 0 else None)
            yield
            store(h, normalise(stats, x_tile))
            yield

        stores = []

        def store(h, w_x):
            for i in range(2):
                done, b = sem(f"store{2 * h + i}"), 2 * h + i
                sp.add(lambda e, b=b, done=done: e.dma_start(
                    out_dram[b].rearrange("(t p) d -> p t d", p=P),
                    x[:, TB * b:TB * b + TB, :]).then_inc(done, 16), w_x[TB * (i + 1) - 1], signal=False)
                stores.append((done, 16))

        w_attn1_const = load_attn1()
        background.append(learned_adjacency())
        background.append(context_keys())
        units = []
        for g in range(NG - 2):
            for b in range(B):
                if b == B - 1:
                    units.append((prepare_group_weights(g + 1), 0))
                units.append((attention_group(b, g), 2))
        g = NG - 2
        units += [(attention_group(0, g), 2), (attention_group(1, g), 2), (attention_group(2, g), 1),
                  (prepare_group_weights(g + 1), 1),
                  (attention_group(0, g + 1), 2), (attention_group(1, g + 1), 2), (attention_group(3, g), 2),
                  (attention_group(2, g + 1), 2), (attention_group(3, g + 1), 2)]
        u_pair, g_pair, v_ring, q1_ring, k1_ring, q1m_ring, ctx1_ring, bi_ring, bi_stat, outT_ring, g1_pair = (
            Ring([]) for _ in range(11))
        memory_experts, zeroed = [], []

        def give(made, *waits):
            for r, filled in made:
                r.slots = filled.slots
                for slot in r.slots:
                    slot.free = list(waits)

        def experts_memory():
            assert "adjacency_done" in ready
            memory0.close()
            memory_experts.append(stage_memory("right"))
            give([(u_pair, pair_ring("u_pair", 2, [P, DC, HALF])), (g_pair, pair_ring("g_pair", 2, [P, DC, HALF]))],
                 *last_so_far())
            yield

        def heads1_memory():
            memory_heads0.close()
            stage_memory()
            read = last_so_far()
            give([(v_ring, ring("v_tok", 2, [P, TB, H1, HS1])), (q1_ring, ring("qT1", 2, [P, H1 // HEADS_PER_TILE, S])),
                  (k1_ring, ring("kT1", 2, [P, H1 // HEADS_PER_TILE, S])),
                  (q1m_ring, ring("q_masked", 2, [P, GH, S]))], *read)
            zeroed.extend(pool.add(lambda e, v=v: e.memset(v.t[...], 0.0), v.free) for v in v_ring.slots)
            yield

        def layer1_memory():
            memory_experts[0].close()
            stage_memory("right")
            give([(ctx1_ring, ring("ctx1", 2, [P, S])), (bi_ring, ring("bilinear", 2, [P, TB, S])),
                  (bi_stat, ring("bi_stat", 2, [P, 3, TB])), (outT_ring, ring("outT", 2, [CTX, S])),
                  (g1_pair, pair_ring("g1_pair", 2, [P, HALF]))], *last_so_far())
            yield

        def by_halves(e):
            return [(e, 0), (e + 1, 0), (e, 1), (e + 1, 1)]

        order = by_halves(0) + [(e, h) for e in range(2, NE - 2) for h in range(NHALF)] + by_halves(NE - 2)
        units[-1] = (units[-1][0], 5)
        units.append((experts_memory(), 0))
        period = {(0, 0): 2, (NE - 1, 1): 2}
        for e, h in order:
            if (e, h) == (NE - 1, 1):
                units.append((heads1_memory(), 0))
            units.append((expert(e, h), period.get((e, h), 1)))
        units.append((project_qkv(0), 2))
        units.append((layer1_memory(), 0))
        for b in range(B):
            for g in range(G1):
                if g == 2 and b + 1 < B:
                    units.append((project_qkv(b + 1), 0))
                units.append((attention1_group(b, g), 2))
        units[-1] = (units[-1][0], 5)
        units += [(ffn(h, m), 1) for h in range(NHALF) for m in range(HT)]
        pipeline(units)
        while background:
            advance()
        for w in stores:
            sp.add(None, w, signal=False)

        block = ctx.enter_context(nc.Block())

        @block.sync
        def _(e):
            sp.play(e)

        @block.tensor
        def _(e):
            pe.play(e)

        @block.scalar
        def _(e):
            act.play(e)

        @block.vector
        def _(e):
            dve.play(e)

        @block.gpsimd
        def _(e):
            pool.play(e)


def rope_table(n, dim):
    inv = (1.0 / np.float32(10000.0) ** (np.arange(0, dim, 2, dtype=np.float32) / np.float32(dim))).astype(np.float32)
    angle = np.arange(n, dtype=np.float32)[:, None] * inv
    cos, sin = np.cos(angle).astype(np.float32), np.sin(angle).astype(np.float32)
    return np.stack([np.concatenate([cos, cos], 1), np.concatenate([-sin, sin], 1)], 1)


def constants():
    q, k = np.arange(P)[:, None], np.arange(S)[None, :]
    mask0 = np.where(k - P > q, np.float32(NEG), np.float32(0))
    rows = np.arange(S).reshape(TB, P).T
    mask1 = np.where(np.arange(S)[None, None, :] > rows[:, :, None], np.float32(-10000.0 * HD1 ** 0.5), np.float32(0))

    def by_tile(t):
        return np.ascontiguousarray(t.reshape(TB, P, *t.shape[1:]).swapaxes(0, 1))

    return {
        "identity": np.eye(P, dtype=np.float32),
        "mask0": mask0.astype(np.float32),
        "mask1": mask1.astype(np.float32),
        "rope0": by_tile(rope_table(S, DR)),
        "rope1": by_tile(rope_table(S, HD1)),
        "row_mask": (np.arange(P)[:, None] // HD1 == np.arange(HEADS_PER_TILE)[None, :]).astype(np.float32),
        "iota": np.broadcast_to(np.arange(NE, dtype=np.float32), (P, NE)).copy(),
    }


def layouts(w):
    q_b = w["L0_attn_q_b_w"].reshape(QLR, NH, DQK)
    kv_b = w["L0_attn_kv_b_w"].reshape(KVLR, NH, DN + DV)
    out = {
        "x": w["x"],
        "xT": w["x"].reshape(T, D).T,
        "ctxT": w["ctx_512"].reshape(T, CTX).T,
        "w_nopeT": q_b[:, :, :DN].transpose(2, 1, 0),
        "w_rot": q_b[:, :, DN:],
        "w_k_latT": kv_b[:, :, :DN].transpose(2, 1, 0),
        "w_v_latT": kv_b[:, :, DN:].transpose(2, 1, 0),
        "w_o": w["L0_attn_o_w"].reshape(NH, DV, D).transpose(1, 0, 2),
        "q_ln": np.stack([w["L0_attn_q_a_ln_w"][0:P], np.tile(w["L0_attn_q_a_ln_w"][P:QLR], 2)], 1),
        "L0_xattn_WqT": w["L0_xattn_Wq"].T,
        "L0_xattn_WkT": w["L0_xattn_Wk"].T,
        "gamma_raw": w["L0_xattn_gamma_raw"].reshape(1),
        "L1_xattn_WkT": w["L1_xattn_W_k"].T,
        "L1_b_col": w["L1_xattn_b_k"].reshape(CTX, 1),
        "bsd_row": w["L0_ffn_bsd"].reshape(1, D),
        "bup_cols": w["L0_ffn_bup"].reshape(E_ROUTED, DC, P).transpose(2, 0, 1),
        "bsu_cols": w["L0_ffn_bsu"].reshape(DC, P).T,
        "bgate_cols": w["L0_ffn_bgate"].reshape(E_ROUTED, DC, P).transpose(2, 0, 1),
        "bsg_cols": w["L0_ffn_bsg"].reshape(DC, P).T,
        "w_gateT": w["L1_ffn_w_gate"].T,
        "w_upT": w["L1_ffn_w_up"].T,
        "w_downT": w["L1_ffn_w_down"].T,
    }
    for name in ("L0_attn_q_a_w", "L0_attn_kv_a_w", "L0_attn_kv_a_ln_w", "L0_ffn_Wr", "L0_ffn_br", "L0_ffn_gate_bias",
                 "L0_ffn_Wup", "L0_ffn_Wgate", "L0_ffn_Wdown", "L0_ffn_bdown", "L0_ffn_Wsu", "L0_ffn_Wsg", "L0_ffn_Wsd",
                 "L1_attn_Wqkv", "L1_attn_bqkv", "L1_attn_Wout", "L1_attn_bout", "L1_xattn_b_k", "L1_xattn_ln_gamma",
                 "L1_xattn_ln_beta"):
        out[name] = w[name]
    return out


def kernel(**inputs):
    from concourse import bacc
    from concourse.bass_utils import run_bass_kernel_spmd

    arrays = layouts({k: np.asarray(v) for k, v in inputs.items()})
    arrays.update(constants())
    arrays = {k: np.ascontiguousarray(v) for k, v in arrays.items()}
    nc = bacc.Bacc("TRN2", target_bir_lowering=False, num_devices=1)
    aps = {k: nc.dram_tensor("in_" + k, v.shape, mybir.dt.from_np(v.dtype), kind="ExternalInput").ap()
           for k, v in arrays.items()}
    out = nc.dram_tensor("out", (B, S, D), F32, kind="ExternalOutput").ap()
    build(nc, aps, out)
    r = run_bass_kernel_spmd(nc, [{"in_" + k: v for k, v in arrays.items()}], core_ids=[0])
    return r.results[0]["out"]
```
